# Optimizing a Trainium2 kernel written in Bass

```python
import numpy as np
import jax
import jax.numpy as jnp

def _softmax(x, axis=-1):
    return jax.nn.softmax(x, axis=axis)

def _gelu(x):
    return jax.nn.gelu(x, approximate=True)

def _silu(x):
    return jax.nn.silu(x)

def _sigmoid(x):
    return jax.nn.sigmoid(x)

def _layernorm(x, axis=-1, eps=1e-05):
    m = jnp.mean(x, axis=axis, keepdims=True)
    v = jnp.var(x, axis=axis, keepdims=True)
    return (x - m) / jnp.sqrt(v + eps)

def _scatter_add(tgt, idx, src, axis=0):
    return tgt.at[idx].add(src)

def _segment_sum(src, seg, n):
    return jax.ops.segment_sum(src, seg, n)
kernel_name = 'mk_decoder_preln_d1_seqx_r4_307986'

def setup_inputs(seed: int=0):
    np.random.seed(seed)
    _w = jnp.asarray

    def _rec_inputs():
        import jax
        import jax.numpy as jnp
        _rk = jax.random.key(seed)
        x = -0.0002928 + 1 * jax.random.normal(jax.random.fold_in(_rk, 1), (16, 100, 256), jnp.float32)
        _lenS = 100 - jax.random.randint(jax.random.fold_in(_rk, 7), (16,), 0, max(1, 100 // 4) + 1, jnp.int32)
        _lenS2 = 361 - jax.random.randint(jax.random.fold_in(_rk, 8), (16,), 0, max(1, 361 // 4) + 1, jnp.int32)
        _ctx_1024P = jax.random.normal(jax.random.fold_in(_rk, 11), (16, 16, 256), jnp.float32)
        _ctx_1024c = jax.random.dirichlet(jax.random.fold_in(_rk, 511), 0.3 * jnp.ones((16,), jnp.float32), (16, 361))
        _ctx_1024t = jnp.einsum('bsk,bkd->bsd', _ctx_1024c, _ctx_1024P)
        _ctx_1024t = _ctx_1024t * jax.lax.rsqrt(jnp.mean(jnp.square(_ctx_1024t)) + 1e-12) * 0.953939
        ctx_1024 = 4.13588e-05 + 0.999923 * (_ctx_1024t + 0.3 * jax.random.normal(jax.random.fold_in(_rk, 611), (16, 361, 256), jnp.float32))
        return (x, ctx_1024)
    x, ctx_1024 = _rec_inputs()

    def _L0_attn_setup():
        import jax, jax.numpy as jnp
        import numpy as np
        B, S, D, H = (2, 512, 256, 16)
        MASK_VAL = -50000.0
        key = jax.random.key(seed)
        k1, k2, k3, k4 = jax.random.split(key, 4)
        s = 1.0 / np.sqrt(D)
        return {'x': jax.random.normal(k1, (B, S, D), dtype=jnp.float32), 'Wq': jax.random.normal(k2, (D, D), dtype=jnp.float32) * s, 'Wkv': jax.random.normal(k3, (D, 2 * D), dtype=jnp.float32) * s, 'Wo': jax.random.normal(k4, (D, D), dtype=jnp.float32) * s}
    _L0_attn_all = _L0_attn_setup()
    _L0_attn_in = {k: v for k, v in _L0_attn_all.items() if k in ('Wq', 'Wkv', 'Wo')}
    del _L0_attn_all

    def _L0_xattn_setup():
        import jax, jax.numpy as jnp
        import numpy as np
        B, S, T = (4, 256, 512)
        HID = 256
        NH = 16
        NKV = 4
        HD = HID // NH
        key = jax.random.key(seed)
        ks = jax.random.split(key, 6)
        scale = 1.0 / np.sqrt(HID)
        return {'x': jax.random.normal(ks[0], (B, S, HID), dtype=jnp.float32), 'context': jax.random.normal(ks[1], (B, T, HID), dtype=jnp.float32), 'Wq': jax.random.normal(ks[2], (NH * HD, HID), dtype=jnp.float32) * scale, 'Wk': jax.random.normal(ks[3], (NKV * HD, HID), dtype=jnp.float32) * scale, 'Wv': jax.random.normal(ks[4], (NKV * HD, HID), dtype=jnp.float32) * scale, 'Wo': jax.random.normal(ks[5], (HID, NH * HD), dtype=jnp.float32) * scale}
    _L0_xattn_all = _L0_xattn_setup()
    _L0_xattn_in = {k: v for k, v in _L0_xattn_all.items() if k in ('Wq', 'Wk', 'Wv', 'Wo')}
    del _L0_xattn_all

    def _L0_ffn_setup():
        import jax, jax.numpy as jnp
        import numpy as np
        B, S, D_MODEL, D_FF = (4, 512, 256, 1024)

        def _quantum_transform(hidden, theta, w_real, w_imag):
            imag = w_imag * jnp.sin(theta + hidden * 0.1)
            quantum_phase = jnp.cos(theta) * w_real + jnp.sin(theta) * w_imag
            return hidden + quantum_phase * imag * 0.1
        key = jax.random.key(seed)
        ks = jax.random.split(key, 8)
        return {'x': jax.random.normal(ks[0], (B, S, D_MODEL), dtype=jnp.float32), 'W1': jax.random.normal(ks[1], (D_MODEL, D_FF), dtype=jnp.float32) * (1.0 / np.sqrt(D_MODEL)), 'b1': jnp.zeros((D_FF,), dtype=jnp.float32), 'quantum_phases': jax.random.normal(ks[2], (D_FF,), dtype=jnp.float32) * (2.0 * np.pi), 'quantum_weights_real': jax.random.normal(ks[3], (D_FF,), dtype=jnp.float32) * 0.1, 'quantum_weights_imag': jax.random.normal(ks[4], (D_FF,), dtype=jnp.float32) * 0.1, 'W2': jax.random.normal(ks[5], (D_FF, D_MODEL), dtype=jnp.float32) * (1.0 / np.sqrt(D_FF)), 'b2': jnp.zeros((D_MODEL,), dtype=jnp.float32)}
    _L0_ffn_all = _L0_ffn_setup()
    _L0_ffn_in = {k: v for k, v in _L0_ffn_all.items() if k in ('W1', 'b1', 'quantum_phases', 'quantum_weights_real', 'quantum_weights_imag', 'W2', 'b2')}
    del _L0_ffn_all
    return {'x': x, 'ctx_1024': ctx_1024, 'L0_attn_Wq': _L0_attn_in['Wq'], 'L0_attn_Wkv': _L0_attn_in['Wkv'], 'L0_attn_Wo': _L0_attn_in['Wo'], 'L0_xattn_Wq': _L0_xattn_in['Wq'], 'L0_xattn_Wk': _L0_xattn_in['Wk'], 'L0_xattn_Wv': _L0_xattn_in['Wv'], 'L0_xattn_Wo': _L0_xattn_in['Wo'], 'L0_ffn_W1': _L0_ffn_in['W1'], 'L0_ffn_b1': _L0_ffn_in['b1'], 'L0_ffn_quantum_phases': _L0_ffn_in['quantum_phases'], 'L0_ffn_quantum_weights_real': _L0_ffn_in['quantum_weights_real'], 'L0_ffn_quantum_weights_imag': _L0_ffn_in['quantum_weights_imag'], 'L0_ffn_W2': _L0_ffn_in['W2'], 'L0_ffn_b2': _L0_ffn_in['b2']}

def reference(x, ctx_1024, L0_attn_Wq, L0_attn_Wkv, L0_attn_Wo, L0_xattn_Wq, L0_xattn_Wk, L0_xattn_Wv, L0_xattn_Wo, L0_ffn_W1, L0_ffn_b1, L0_ffn_quantum_phases, L0_ffn_quantum_weights_real, L0_ffn_quantum_weights_imag, L0_ffn_W2, L0_ffn_b2):
    import jax
    import jax.numpy as jnp

    def _L0_attn_ref(x, Wq, Wkv, Wo):
        import jax, jax.numpy as jnp
        import numpy as np
        B, S, D, H = (2, 512, 256, 16)
        MASK_VAL = -50000.0
        b, sl, d = x.shape
        h = H
        hd = d // h
        scale = hd ** (-0.5)
        q = x @ Wq
        kv = x @ Wkv
        k, v = jnp.split(kv, 2, axis=-1)
        q = q.reshape(b, sl, h, hd).transpose(0, 2, 1, 3)
        k = k.reshape(b, sl, h, hd).transpose(0, 2, 1, 3)
        v = v.reshape(b, sl, h, hd).transpose(0, 2, 1, 3)
        dots = jnp.einsum('bhid,bhjd->bhij', q * scale, k)
        causal = jnp.tril(jnp.ones((sl, sl), dtype=bool))
        dots = jnp.where(causal, dots, MASK_VAL)
        attn = jax.nn.softmax(dots, axis=-1)
        out = jnp.einsum('bhij,bhjd->bihd', attn, v).reshape(b, sl, d)
        return out @ Wo

    def _L0_xattn_ref(x, context, Wq, Wk, Wv, Wo):
        import jax, jax.numpy as jnp
        import numpy as np
        B, S, T = (4, 256, 512)
        HID = 256
        NH = 16
        NKV = 4
        HD = HID // NH
        Bx, Sx, _ = x.shape
        Tx = context.shape[1]
        rep = NH // NKV
        q = (x @ Wq.T).reshape(Bx, Sx, NKV, rep, HD)
        k = (context @ Wk.T).reshape(Bx, Tx, NKV, HD)
        v = (context @ Wv.T).reshape(Bx, Tx, NKV, HD)
        scale = 1.0 / jnp.sqrt(jnp.asarray(HD, dtype=q.dtype))
        scores = jnp.einsum('bsgrd,btgd->bgrst', q, k) * scale
        attn = jax.nn.softmax(scores, axis=-1)
        out = jnp.einsum('bgrst,btgd->bsgrd', attn, v)
        out = out.reshape(Bx, Sx, NH * HD)
        return out @ Wo.T

    def _L0_ffn_ref(x, W1, b1, quantum_phases, quantum_weights_real, quantum_weights_imag, W2, b2):
        import jax, jax.numpy as jnp
        import numpy as np
        B, S, D_MODEL, D_FF = (4, 512, 256, 1024)

        def _quantum_transform(hidden, theta, w_real, w_imag):
            imag = w_imag * jnp.sin(theta + hidden * 0.1)
            quantum_phase = jnp.cos(theta) * w_real + jnp.sin(theta) * w_imag
            return hidden + quantum_phase * imag * 0.1
        hidden = jnp.einsum('bsd,df->bsf', x, W1) + b1
        q = _quantum_transform(hidden, quantum_phases, quantum_weights_real, quantum_weights_imag)
        act = jax.nn.relu(q)
        return jnp.einsum('bsf,fd->bsd', act, W2) + b2
    x = x + _L0_attn_ref(_layernorm(x, axis=-1), L0_attn_Wq, L0_attn_Wkv, L0_attn_Wo)
    x = x + _L0_xattn_ref(_layernorm(x, axis=-1), ctx_1024, L0_xattn_Wq, L0_xattn_Wk, L0_xattn_Wv, L0_xattn_Wo)
    x = x + _L0_ffn_ref(_layernorm(x, axis=-1), L0_ffn_W1, L0_ffn_b1, L0_ffn_quantum_phases, L0_ffn_quantum_weights_real, L0_ffn_quantum_weights_imag, L0_ffn_W2, L0_ffn_b2)
    return x

_drawn_inputs = setup_inputs


def setup_inputs(seed=0):
    import zlib

    import numpy as np

    out = dict(_drawn_inputs(seed))
    spreads = {'L0_ffn_b1': (0.0, 0.1), 'L0_ffn_b2': (0.0, 0.1)}
    factors = {'L0_ffn_quantum_phases': 8.0,
     'L0_ffn_quantum_weights_real': 40.077,
     'L0_ffn_quantum_weights_imag': 8.0}
    for name, (base, spread) in spreads.items():
        noise = np.random.default_rng([zlib.crc32(name.encode()), seed]).standard_normal(out[name].shape)
        drawn = base * np.exp(spread * noise) if base else spread * noise
        out[name] = jnp.asarray(drawn.astype(out[name].dtype))
    for name, factor in factors.items():
        out[name] = (out[name] * factor).astype(out[name].dtype)
    return out
```

```python
import numpy as np
import concourse.bass as bass
from concourse import mybir
from contextlib import ExitStack

F32 = mybir.dt.float32
BF16 = mybir.dt.bfloat16
ACT = mybir.ActivationFunctionType
ALU = mybir.AluOpType
AX = mybir.AxisListType

B, S, D, H, T, F = 16, 100, 256, 16, 361, 1024
HD = D // H
G = 4
R = H // G
KT = D // 128
PAIR = 2
NP = B // PAIR
N = PAIR * S
NTERM = 6
KROWS = NTERM * HD
KM = KROWS + 3
Q_TERM = (0, 0, 1, 0, 1, 2)
K_TERM = (0, 1, 0, 2, 1, 0)
TT = (T + 127) // 128
TROWS = [min(128, T - 128 * j) for j in range(TT)]
VW = 32
RS = R * S
SCALE = HD ** -0.5
MASKED = -262144.0
EPS = 1e-5
FT = F // 128
QB = 4
NQ = B // QB
NTOK = QB * S
TWO_PI = float(np.float32(2 * np.pi))
INV_TWO_PI = float(np.float32(1 / (2 * np.pi)))
PI_BELOW = 3.1415925
ROUND = 1.5 * 2.0 ** 23
C1 = 6.28125
C2 = float(2 * np.pi - 6.28125)
COEF_STEPS, COEF_LAST = 10, 5

PJ_USES = [("kv0", "self"), ("kv1", "self"), ("self_max", "self"), ("cross_max", "cross"),
           ("self_t1_0", "self"), ("self_t1_1", "self"), ("xT", "next"), ("q", "next"), ("self_t2", "self"),
           ("k", "next"), ("self_o", "self"), ("v", "next"), ("x1T", "self"), ("qx", "self"),
           ("cross_t1_0", "cross"), ("vx0", "self"), ("vx1", "self"), ("cross_t1_1", "cross"),
           ("cross_t2", "cross"), ("cross_o", "cross")]
MX_USES = [(f"self{u}", "self") for u in range(PAIR * G)] + [(f"cross{u}", "cross") for u in range(PAIR * H)]
SC_USES = [(f"self{u}", "self") for u in range(PAIR * G)] + [(f"cross{u}", "cross") for u in range(PAIR * TT * G)]


def active(i):
    return [p for p, on in (("next", i < NP - 1), ("self", 0 <= i < NP), ("cross", i >= 1)) if on]


def uses_before(uses, i):
    return sum(sum(part in active(m) for _, part in uses) for m in range(-1, i))


def use(uses, step, i):
    m = i if isinstance(i, int) else 1
    names = [s for s, part in uses if part in active(m)]
    n = uses_before(uses, m) + names.index(step)
    if isinstance(i, int):
        return n % 2, n // 2
    return n % 2, (i - 1) * (len(uses) // 2) + n // 2


def decoder(nc, x, ctxT, wq, wkv, wo, cwqT, cwkvT, cwoT, w1, coefs, w2, b2, ident, mask, out):
    ctx = ExitStack()
    with ctx:
        def sb(name, shape, dt=F32):
            return ctx.enter_context(nc.sbuf_tensor(name, shape, dt))

        def sem(name):
            return ctx.enter_context(nc.semaphore(name))

        qs_dram = nc.dram_tensor("qs_dram", [D, 3, N], BF16, kind="Internal").ap()
        ks_dram = nc.dram_tensor("ks_dram", [D, 3, N], BF16, kind="Internal").ap()
        qx_dram = nc.dram_tensor("qx_dram", [D, 3, N], BF16, kind="Internal").ap()
        kx_dram = nc.dram_tensor("kx_dram", [G * HD, 3, PAIR * T], BF16, kind="Internal").ap()

        ident_sb = sb("ident_sb", [128, 128])
        ident_bf = sb("ident_bf", [128, 128], BF16)
        mask_bf = sb("mask_bf", [S, R, S], BF16)
        maskT_bf = sb("maskT_bf", [S, R, S], BF16)
        mask_f = sb("mask_f", [S, 2, S])
        wq_sb = sb("wq_sb", [128, KT, D])
        wkv_sb = sb("wkv_sb", [128, KT, 2 * D])
        wo_sb = sb("wo_sb", [128, KT, D])
        cwq_sb = sb("cwq_sb", [128, KT, D])
        cwkv_sb = sb("cwkv_sb", [128, KT, 2 * G * HD])
        cwo_sb = sb("cwo_sb", [128, KT, D])
        w1_sb = sb("w1_sb", [128, KT, F])
        w2_sb = sb("w2_sb", [128, FT, D])
        b2_sb = sb("b2_sb", [S, D])
        half_sb = sb("half_sb", [S, QB])

        xl = sb("xl", [S, PAIR, D])
        xr = sb("xr", [S, PAIR, D])
        x1 = sb("x1", [S, PAIR, D])
        x1r = sb("x1r", [S, PAIR, D])
        x2 = sb("x2", [S, PAIR, D])
        x2_all = sb("x2_all", [S, B, D])
        stats = [sb(f"stats{n}", [S, QB, 6]) for n in range(3)]
        moments = [sb(f"moments{n}", [S, QB, 2]) for n in range(3)]
        vareps = [sb(f"vareps{n}", [S, QB]) for n in range(3)]
        rstd = [sb(f"rstd{n}", [S, QB]) for n in range(3)]
        xn1 = sb("xn1", [S, PAIR, D])
        xn2 = sb("xn2", [S, PAIR, D])
        xT = sb("xT", [128, KT, N])
        x1T = sb("x1T", [128, KT, N])
        ctxT_sb = sb("ctxT_sb", [128, KT, PAIR, T])
        q_parts = sb("q_parts", [128, KT, 3, N], BF16)
        k_parts = sb("k_parts", [128, KT, 3, N], BF16)
        qx_parts = sb("qx_parts", [128, KT, 3, N], BF16)
        kx_parts = sb("kx_parts", [G * HD, 3, PAIR, T], BF16)
        q_rest = sb("q_rest", [128, KT, N])
        k_rest = sb("k_rest", [128, KT, N])
        qx_rest = sb("qx_rest", [128, KT, N])
        kx_rest = sb("kx_rest", [G * HD, PAIR, T])
        q_stack = sb("q_stack", [128, H, N], BF16)
        k_stack = sb("k_stack", [128, H, N], BF16)
        qx_stack = sb("qx_stack", [128, H, N], BF16)
        kx_stack = sb("kx_stack", [128, G, PAIR, T], BF16)
        vT = sb("vT", [128, PAIR, T])
        v_sb = sb("v_sb", [S, PAIR * H, VW])
        vx_sb = sb("vx_sb", [128, PAIR, TT, G, VW])
        max_s = sb("max_s", [S, H, PAIR])
        max_x = sb("max_x", [S, H, PAIR])
        ms_parts = sb("ms_parts", [H * PAIR, 3, S], BF16)
        mx_parts = sb("mx_parts", [H * PAIR, 3, S], BF16)
        ms_rest = sb("ms_rest", [H * PAIR, S])
        mx_rest = sb("mx_rest", [H * PAIR, S])
        p_self = sb("p_self", [128, PAIR * G, RS])
        p_cross = sb("p_cross", [128, PAIR * TT * G, RS])
        outT_s = sb("outT_s", [128, PAIR, RS])
        outT_x = sb("outT_x", [128, PAIR, RS])
        recip_s = sb("recip_s", [S, PAIR, R, G])
        recip_x = sb("recip_x", [S, PAIR, R, G])
        o_s = sb("o_s", [S, PAIR, D])
        o_x = sb("o_x", [S, PAIR, D])
        oT_s = sb("oT_s", [128, KT, N])
        oT_x = sb("oT_x", [128, KT, N])

        xn3 = sb("xn3", [S, QB, D])
        x3T = sb("x3T", [128, KT, NTOK])
        x2b = sb("x2b", [S, QB, D])
        coef_in = sb("coef_in", [128, 4, FT])
        coef = sb("coef", [128, 8, FT])
        ANG, COSANG, N1, N2, SINV, COSV, AMP, BIAS = range(8)
        y_sb, n_sb, m_sb, r_sb, rc_sb, sin_sb = (p_cross[:, 4 * n:4 * n + 4, :] for n in range(6))
        z_sb = p_self[:, :4, :]
        stack_f32 = q_stack[:].rearrange("p h n -> p (h n)").bitcast(F32).rearrange("p (f n) -> p f n", n=NTOK)
        act_sb = [p_self[:, 4 + f, :] for f in range(4)] + [stack_f32[:, f, :] for f in range(4)]
        fin = sb("fin", [S, QB, D])

        mx = [ctx.enter_context(nc.psum_tensor(f"mx{n}", [128, 512], F32)) for n in range(2)]
        sc = [ctx.enter_context(nc.psum_tensor(f"sc{n}", [128, 512], F32)) for n in range(2)]
        ot = [ctx.enter_context(nc.psum_tensor(f"ot{n}", [128, 512], F32)) for n in range(2)]
        pj = [ctx.enter_context(nc.psum_tensor(f"pj{n}", [128, 512], F32)) for n in range(2)]
        hid = [mx[0], mx[1], sc[0], sc[1]]

        first_in = sem("first_in")
        attn_weights_in = sem("attn_weights_in")
        ffn_weights_in = sem("ffn_weights_in")
        coefs_in = sem("coefs_in")
        waits_carried = sem("waits_carried")
        consts_set = sem("consts_set")
        masks_set = sem("masks_set")
        xl_in = sem("xl_in")
        xr_in = sem("xr_in")
        ctx_in = sem("ctx_in")
        ln_stats = [sem(f"ln{n}_stats") for n in range(3)]
        ln_moments = [sem(f"ln{n}_moments") for n in range(3)]
        ln_eps = [sem(f"ln{n}_eps") for n in range(3)]
        ln_rstd = [sem(f"ln{n}_rstd") for n in range(3)]
        xn_ready = [sem(f"xn{n}_ready") for n in range(3)]
        pj_full = [sem(f"pj_full{n}") for n in range(2)]
        pj_free = [sem(f"pj_free{n}") for n in range(2)]
        mx_full = [sem(f"mx_full{n}") for n in range(2)]
        mx_free = [sem(f"mx_free{n}") for n in range(2)]
        sc_full = [sem(f"sc_full{n}") for n in range(2)]
        sc_free = [sem(f"sc_free{n}") for n in range(2)]
        ot_full = [sem(f"ot_full{n}") for n in range(2)]
        ot_free = [sem(f"ot_free{n}") for n in range(2)]
        split = ("q", "k", "qx", "kx", "self_max", "cross_max")
        high_ready = {n: sem(f"{n}_high") for n in split}
        mid_ready = {n: sem(f"{n}_mid") for n in split}
        low_ready = {n: sem(f"{n}_low") for n in split}
        parts_out = {n: sem(f"{n}_out") for n in split[:4]}
        self_stacks_in = sem("self_stacks_in")
        cross_stacks_in = sem("cross_stacks_in")
        maxima_in = {n: sem(f"{n}_in") for n in split[4:]}
        recip_ready = {k: sem(f"{k}_recip") for k in ("self", "cross")}
        x1r_ready = sem("x1r_ready")
        x2_kept = sem("x2_kept")
        coef_step = sem("coef_step")
        coef_sin = sem("coef_sin")
        x3T_full = sem("x3T_full")
        x3T_ready = sem("x3T_ready")
        hid_full = sem("hid_full")
        y_ready = sem("y_ready")
        n_ready = sem("n_ready")
        m_ready = sem("m_ready")
        r_ready = sem("r_ready")
        rc_ready = sem("rc_ready")
        sin_ready = sem("sin_ready")
        z_ready = sem("z_ready")
        act_ready = sem("act_ready")
        acc_full = sem("acc_full")
        fin_ready = sem("fin_ready")
        x2b_ready = sem("x2b_ready")
        out_done = sem("out_done")

        block = ctx.enter_context(nc.Block())
        NSETS = 5
        NFIRST, NATTN, NFFN = 5, 3, 3
        STACKED = 16 * 2 * NTERM
        SENT = 16 * 3

        def at_least(eng, s, n):
            if not isinstance(n, int) or n > 0:
                eng.wait_ge(s, n)

        def alone(eng):
            eng.sem_inc(waits_carried, 1)

        def filled(eng, uses, full, step, i):
            n, before = use(uses, step, i)
            eng.wait_ge(full[n], before + 1)
            return n

        def copied(eng, step, i):
            n, before = use(PJ_USES, step, i)
            eng.wait_ge(pj_free[n], before + 1)

        def on(part, i):
            return not isinstance(i, int) or part in active(i)

        def passes(eng, body):
            body(0)
            with eng.Fori(1, NP - 1) as i:
                body(i)
            body(NP - 1)
            body(NP)

        def ot_uses(kind, p):
            if kind == "self":
                return 0 if isinstance(p, int) and p == 0 else 2 * p - 1
            return 2 * p + 1 if isinstance(p, int) and p == NP - 1 else 2 * p + 2

        @block.sync
        def _(sp):
            def wait(s, n):
                at_least(sp, s, n)
                alone(sp)

            def wait_copied(step, i):
                copied(sp, step, i)
                alone(sp)

            def rows(b0, n):
                return x[bass.ds(b0, n)].rearrange("b s d -> s b d")

            def load_ctx(p):
                for b in range(PAIR):
                    sp.dma_start(ctxT_sb[:, :, b, :], ctxT[PAIR * p + b].rearrange("(k p) t -> p k t", p=128)
                                 if isinstance(p, int) else
                                 ctxT[bass.ds(PAIR * p + b, 1)].rearrange("o (k p) t -> p (o k) t", p=128)).then_inc(ctx_in, 16)

            def parts_to_dram(name, parts, dram, p):
                wait(low_ready[name], p + 1)
                sp.dma_start(dram.rearrange("(m p) t s -> p m (t s)", p=128), parts[:].rearrange("p m t s -> p m (t s)")).then_inc(parts_out[name], 16)

            def stack(dst, dram, terms, name, p, done):
                wait(parts_out[name], 16 * (p + 1))
                for n, t in enumerate(terms):
                    sp.dma_start(dst[n * HD:(n + 1) * HD], dram[:, t, :].rearrange("(h d) s -> d h s", d=HD)).then_inc(done, 16)

            def self_stacks(p):
                parts_to_dram("q", q_parts, qs_dram, p)
                parts_to_dram("k", k_parts, ks_dram, p)
                stack(q_stack[:], qs_dram, Q_TERM, "q", p, self_stacks_in)
                stack(k_stack[:], ks_dram, K_TERM, "k", p, self_stacks_in)

            def send_maxima(name, parts, dst, p):
                wait(low_ready[name], p + 1)
                for t in range(3):
                    sp.dma_start(dst[KROWS + t:KROWS + t + 1].rearrange("p h n -> p (h n)"), parts[:, t, :]).then_inc(maxima_in[name], 16)

            def body(i):
                if on("next", i):
                    wait(xn_ready[0], PAIR * (i + 1))
                    sp.dma_start(xl[:], rows(PAIR * (i + 1), PAIR)).then_inc(xl_in, 16)
                if on("self", i):
                    wait(low_ready["kx"], PAIR * (i + 1))
                    wait(cross_stacks_in, STACKED * i)
                    sp.dma_start(kx_dram.rearrange("f t n -> f (t n)"), kx_parts[:64].rearrange("p t b n -> p (t b n)")).then_inc(parts_out["kx"], 16)
                    if on("next", i):
                        load_ctx(i + 1)
                    send_maxima("self_max", ms_parts, q_stack, i)
                if on("cross", i):
                    send_maxima("cross_max", mx_parts, qx_stack, i - 1)
                if on("self", i):
                    sp.dma_start(xr[:], rows(PAIR * i, PAIR)).then_inc(xr_in, 16)
                if on("next", i):
                    self_stacks(i + 1)
                if on("self", i):
                    parts_to_dram("qx", qx_parts, qx_dram, i)
                    if on("cross", i):
                        wait(ot_free[1], ot_uses("cross", i - 1) + 1)
                    stack(qx_stack[:], qx_dram, Q_TERM, "qx", i, cross_stacks_in)
                    stack(kx_stack[:].rearrange("p g b n -> p g (b n)"), kx_dram, K_TERM, "kx", i, cross_stacks_in)
                if on("cross", i):
                    wait_copied("cross_o", i)
                    sp.dma_start(x2_all[:, bass.ds(PAIR * (i - 1), PAIR), :], x2[:]).then_inc(x2_kept, 16)

            def weights(pairs, done):
                for dst, src in pairs:
                    sp.dma_start(dst[:], src.rearrange("(k p) n -> p k n", p=128)).then_inc(done, 16)

            sp.sem_inc(x2_kept, 16)
            sp.sem_inc(out_done, 16 * 2)
            sp.dma_start(xl[:], rows(0, PAIR)).then_inc(xl_in, 16)
            sp.dma_start(ident_sb[:], ident).then_inc(first_in, 16)
            sp.dma_start(mask_f[:], mask).then_inc(first_in, 16)
            weights(((wq_sb, wq), (wkv_sb, wkv), (cwkv_sb, cwkvT)), first_in)
            load_ctx(0)
            weights(((wo_sb, wo), (cwq_sb, cwqT), (cwo_sb, cwoT)), attn_weights_in)
            self_stacks(0)
            weights(((w1_sb, w1), (w2_sb, w2)), ffn_weights_in)
            sp.dma_start(b2_sb[:], b2.partition_broadcast(S)).then_inc(ffn_weights_in, 16)
            sp.dma_start(coef_in[:], coefs).then_inc(coefs_in, 16)
            passes(sp, body)

            def store(q):
                for half in range(2):
                    wait(fin_ready, 2 * q + half + 1)
                    sp.dma_start(out[bass.ds(QB * q + 2 * half, 2)].rearrange("b s d -> s b d"), fin[:, 2 * half:2 * half + 2]).then_inc(out_done, 16)
            with sp.Fori(0, NQ) as q:
                store(q)
            wait(out_done, 16 * 2 * (NQ + 1))

        @block.tensor
        def _(pe):
            def bank(step, i):
                n, before = use(PJ_USES, step, i)
                at_least(pe, pj_free[n], before)
                return pj[n], pj_full[n]

            def transpose_rows(step, i, src):
                into, full = bank(step, i)
                for k in range(KT):
                    for b in range(PAIR):
                        last = nc.tensor.transpose(into[:, k * N + b * S:k * N + (b + 1) * S], src[:, b, k * 128:(k + 1) * 128], ident_sb[:S, :S])
                last.then_inc(full, 1)

            def project_T(step, i, w, srcT, read_step):
                into, full = bank(step, i)
                copied(pe, read_step, i)
                for m in range(KT):
                    for k in range(KT):
                        last = nc.tensor.matmul(into[:, m * N:(m + 1) * N], w[:, k, m * 128:(m + 1) * 128], srcT[:, k, :], start=(k == 0), stop=(k == KT - 1))
                last.then_inc(full, 1)

            def project_rows(step, i, w, srcT, read_step):
                into, full = bank(step, i)
                copied(pe, read_step, i)
                for b in range(PAIR):
                    for k in range(KT):
                        last = nc.tensor.matmul(into[:S, b * D:(b + 1) * D], srcT[:, k, b * S:(b + 1) * S], w[:, k, :], start=(k == 0), stop=(k == KT - 1))
                last.then_inc(full, 1)

            def kv_cross(i):
                pe.wait_ge(ctx_in, 16 * PAIR * (i + 1))
                for b in range(PAIR):
                    into, full = bank(f"kv{b}", i)
                    for k in range(KT):
                        last = nc.tensor.matmul(into[:, :T], cwkv_sb[:, k, :], ctxT_sb[:, k, b, :], start=(k == 0), stop=(k == KT - 1))
                    last.then_inc(full, 1)

            def v_cross(i, b):
                copied(pe, f"kv{b}", i)
                into, full = bank(f"vx{b}", i)
                alone(pe)
                for j in range(TT):
                    last = nc.tensor.transpose(into[:TROWS[j], j * 64:(j + 1) * 64], vT[64:, b, j * 128:j * 128 + TROWS[j]], ident_sb[64:, 64:])
                last.then_inc(full, 1)

            def self_rows(i):
                pe.wait_ge(self_stacks_in, STACKED * (i + 1))
                for u in range(PAIR * G):
                    b, g = divmod(u, G)
                    n, before = use(MX_USES, f"self{u}", i)
                    at_least(pe, mx_free[n], before)
                    nc.tensor.matmul(mx[n][:S, :RS], ident_bf[:S, :S], mask_bf[:].rearrange("q h k -> q (h k)"), start=True, stop=False, skip_group_check=True)
                    for r in range(R):
                        h = g * R + r
                        last = nc.tensor.matmul(mx[n][:S, r * S:(r + 1) * S], q_stack[:KROWS, h, b * S:(b + 1) * S],
                                                k_stack[:KROWS, h, b * S:(b + 1) * S], start=False, stop=(r == R - 1), skip_group_check=True)
                    last.then_inc(mx_full[n], 1)

            def cross_rows(i):
                pe.wait_ge(cross_stacks_in, STACKED * i)
                for u in range(PAIR * H):
                    b, h = divmod(u, H)
                    n, before = use(MX_USES, f"cross{u}", i)
                    at_least(pe, mx_free[n], before)
                    nc.tensor.matmul(mx[n][:S, :T], qx_stack[:KROWS, h, b * S:(b + 1) * S], kx_stack[:KROWS, h // R, b, :],
                                     start=True, stop=True).then_inc(mx_full[n], 1)

            def maxima_T(step, i, src, last_units):
                into, full = bank(step, i)
                for u in last_units:
                    n, before = use(MX_USES, u, i)
                    pe.wait_ge(mx_free[n], before + 1)
                nc.tensor.transpose(into[:H * PAIR, :S], src[:].rearrange("s h b -> s (h b)"), ident_sb[:S, :S]).then_inc(full, 1)

            def self_keys(i):
                pe.wait_ge(maxima_in["self_max"], SENT * (i + 1))

                def scores(u):
                    b, g = divmod(u, G)
                    n, before = use(SC_USES, f"self{u}", i)
                    at_least(pe, sc_free[n], before)
                    nc.tensor.matmul(sc[n][:S, :RS], ident_bf[:S, :S], maskT_bf[:].rearrange("k h q -> k (h q)"), start=True, stop=False, skip_group_check=True)
                    for r in range(R):
                        h = g * R + r
                        last = nc.tensor.matmul(sc[n][:S, r * S:(r + 1) * S], k_stack[:KM, h, b * S:(b + 1) * S],
                                                q_stack[:KM, h, b * S:(b + 1) * S], start=False, stop=(r == R - 1), skip_group_check=True)
                    last.then_inc(sc_full[n], 1)

                def values(u):
                    b, g = divmod(u, G)
                    n, before = use(SC_USES, f"self{u}", i)
                    pe.wait_ge(sc_free[n], before + 1)
                    if g == 0:
                        at_least(pe, ot_free[b], ot_uses("self", i))
                    for r in range(R):
                        last = nc.tensor.matmul(ot[b][g * VW:(g + 1) * VW, r * S:(r + 1) * S], v_sb[:, b * H + g * R + r, :],
                                                p_self[:S, u, r * S:(r + 1) * S], start=True, stop=True)
                    if g == G - 1:
                        last.then_inc(ot_full[b], 1)

                for u in range(PAIR * G + 1):
                    if u < PAIR * G:
                        scores(u)
                    if u >= 1:
                        values(u - 1)

            def cross_keys(i, b):
                if b == 0:
                    pe.wait_ge(maxima_in["cross_max"], SENT * i)

                def scores(j, g):
                    n, before = use(SC_USES, f"cross{(b * TT + j) * G + g}", i)
                    at_least(pe, sc_free[n], before)
                    nc.tensor.matmul(sc[n][:TROWS[j], :RS].rearrange("p (r s) -> p r s", r=R), kx_stack[:KM, g, b, j * 128:j * 128 + TROWS[j]],
                                     qx_stack[:KM, g * R:(g + 1) * R, b * S:(b + 1) * S], start=True, stop=True).then_inc(sc_full[n], 1)

                def values(j, g):
                    u = (b * TT + j) * G + g
                    n, before = use(SC_USES, f"cross{u}", i)
                    pe.wait_ge(sc_free[n], before + 1)
                    last = nc.tensor.matmul(ot[b][g * VW:(g + 1) * VW, :RS], vx_sb[:TROWS[j], b, j, g, :], p_cross[:TROWS[j], u, :],
                                            start=(j == 0), stop=(j == TT - 1))
                    if j == TT - 1 and g == G - 1:
                        last.then_inc(ot_full[b], 1)

                units = [(j, g) for j in range(TT) for g in range(G)]
                for n, (j, g) in enumerate(units):
                    scores(j, g)
                    if n % G == 1 and n > G:
                        if n == G + 1:
                            pe.wait_ge(ot_free[b], ot_uses("cross", i - 1))
                        for m in range(n - 1 - G, n - 1):
                            values(*units[m])
                for m in range(len(units) - G, len(units)):
                    values(*units[m])

            def heads_to_rows(kind, i, b, outT, before):
                into, full = bank(f"{kind}_t1_{b}", i)
                pe.wait_ge(ot_free[b], before + 1)
                for r in range(R):
                    last = nc.tensor.transpose(into[:S, r * 128:(r + 1) * 128], outT[:, b, r * S:(r + 1) * S], ident_sb[:])
                last.then_inc(full, 1)

            def body(i):
                if on("self", i):
                    self_rows(i)
                    kv_cross(i)
                    maxima_T("self_max", i, max_s, (f"self{PAIR * G - 2}", f"self{PAIR * G - 1}"))
                if on("cross", i):
                    cross_rows(i)
                if on("self", i):
                    self_keys(i)
                if on("cross", i):
                    maxima_T("cross_max", i, max_x, (f"cross{PAIR * H - 2}", f"cross{PAIR * H - 1}"))
                if on("self", i):
                    for b in range(PAIR):
                        heads_to_rows("self", i, b, outT_s, ot_uses("self", i))
                if on("next", i):
                    pe.wait_ge(xn_ready[0], PAIR * (i + 2))
                    transpose_rows("xT", i, xn1)
                    project_T("q", i, wq_sb, xT, "xT")
                if on("self", i):
                    for b in range(PAIR):
                        copied(pe, f"self_t1_{b}", i)
                    transpose_rows("self_t2", i, o_s)
                if on("next", i):
                    project_T("k", i, wkv_sb, xT, "xT")
                if on("self", i):
                    project_rows("self_o", i, wo_sb, oT_s, "self_t2")
                if on("next", i):
                    project_rows("v", i, wkv_sb[:, :, D:], xT, "xT")
                if on("cross", i):
                    cross_keys(i, 0)
                if on("self", i):
                    pe.wait_ge(xn_ready[1], PAIR * (i + 1))
                    transpose_rows("x1T", i, xn2)
                    project_T("qx", i, cwq_sb, x1T, "x1T")
                if on("cross", i):
                    cross_keys(i, 1)
                    heads_to_rows("cross", i, 0, outT_x, ot_uses("cross", i - 1))
                if on("self", i):
                    for b in range(PAIR):
                        v_cross(i, b)
                if on("cross", i):
                    heads_to_rows("cross", i, 1, outT_x, ot_uses("cross", i - 1))
                    for b in range(PAIR):
                        copied(pe, f"cross_t1_{b}", i)
                    transpose_rows("cross_t2", i, o_x)
                    project_rows("cross_o", i, cwo_sb, oT_x, "cross_t2")

            pe.wait_ge(first_in, 16 * NFIRST)
            pe.wait_ge(consts_set, NSETS)
            pe.wait_ge(masks_set, 1)
            pe.wait_ge(xn_ready[0], PAIR)
            transpose_rows("xT", -1, xn1)
            project_T("q", -1, wq_sb, xT, "xT")
            project_T("k", -1, wkv_sb, xT, "xT")
            project_rows("v", -1, wkv_sb[:, :, D:], xT, "xT")
            pe.wait_ge(attn_weights_in, 16 * NATTN)
            passes(pe, body)

            pe.wait_ge(ffn_weights_in, 16 * NFFN)
            for n in range(2):
                pe.wait_ge(mx_free[n], uses_before(MX_USES, NP + 1) // 2)
                pe.wait_ge(sc_free[n], uses_before(SC_USES, NP + 1) // 2)
                pe.wait_ge(ot_free[n], 2 * NP)
                pe.wait_ge(pj_free[n], (uses_before(PJ_USES, NP + 1) + 1 - n) // 2)

            def hidden(q, f):
                if f == 0:
                    pe.wait_ge(xn_ready[2], QB * (q + 1))
                    for k in range(KT):
                        for b in range(QB):
                            last = nc.tensor.transpose(pj[k][:, b * S:(b + 1) * S], xn3[:, b, k * 128:(k + 1) * 128], ident_sb[:S, :S])
                        last.then_inc(x3T_full, 1)
                    pe.wait_ge(x3T_ready, KT * (q + 1))
                at_least(pe, z_ready, FT * q + f - 3)
                for k in range(KT):
                    last = nc.tensor.matmul(hid[f % 4][:, :NTOK], w1_sb[:, k, f * 128:(f + 1) * 128], x3T[:, k, :], start=(k == 0), stop=(k == KT - 1))
                last.then_inc(hid_full, 1)

            def output(q, f):
                pe.wait_ge(act_ready, FT * q + f + 1)
                if f == 0:
                    at_least(pe, fin_ready, 2 * q)
                for b in range(QB):
                    last = nc.tensor.matmul(ot[b // 2][:S, (b % 2) * D:(b % 2 + 1) * D], act_sb[f][:, b * S:(b + 1) * S], w2_sb[:, f, :],
                                            start=(f == 0 and b % 2 == 0), stop=(f == FT - 1 and b % 2 == 1), skip_group_check=True)
                    if f == FT - 1 and b % 2 == 1:
                        last.then_inc(acc_full, 1)

            LAG = 3
            for f in range(FT):
                hidden(0, f)
                if f >= LAG:
                    output(0, f - LAG)
            with pe.Fori(1, NQ) as q:
                for f in range(FT):
                    hidden(q, f)
                    if f >= LAG:
                        output(q, f - LAG)
                    else:
                        output(q - 1, FT + f - LAG)
            for f in range(FT - LAG, FT):
                output(NQ - 1, f)

        @block.scalar
        def _(act):
            def copy_T(step, i, dst):
                n = filled(act, PJ_USES, pj_full, step, i)
                nc.scalar.copy(dst[:].rearrange("p k n -> p (k n)"), pj[n][:, :KT * N]).then_inc(pj_free[n], 1)

            def high(step, i, name, parts, p):
                n = filled(act, PJ_USES, pj_full, step, i)
                at_least(act, parts_out[name], 16 * p)
                nc.scalar.copy(parts[:, :, 0, :], pj[n][:, :KT * N].rearrange("p (m n) -> p m n", m=KT)).then_inc(high_ready[name], 1)

            def max_high(name, i, parts):
                n = filled(act, PJ_USES, pj_full, name, i)
                nc.scalar.copy(parts[:, 0, :], pj[n][:H * PAIR, :S]).then_inc(high_ready[name], 1)

            def copy_v(i):
                n = filled(act, PJ_USES, pj_full, "v", i)
                nc.scalar.copy(v_sb[:, :, :HD], pj[n][:S, :].rearrange("s (h d) -> s h d", d=HD)).then_inc(pj_free[n], 1)

            def copy_kv(i):
                at_least(act, parts_out["kx"], 16 * i)
                for b in range(PAIR):
                    n = filled(act, PJ_USES, pj_full, f"kv{b}", i)
                    nc.scalar.copy(vT[64:, b, :], pj[n][64:, :T])
                    nc.scalar.copy(kx_parts[:64, 0, b, :], pj[n][:64, :T]).then_inc(high_ready["kx"], 1)

            def copy_vx(i):
                for b in range(PAIR):
                    n = filled(act, PJ_USES, pj_full, f"vx{b}", i)
                    v = pj[n][:, :TT * 64].rearrange("t (j g d) -> t j g d", g=G, d=HD)
                    nc.scalar.copy(vx_sb[:, b, 0, :, :HD], v[:, 0])
                    nc.scalar.copy(vx_sb[:, b, 1, :, :HD], v[:, 1])
                    nc.scalar.copy(vx_sb[:TROWS[2], b, 2, :, :HD], v[:TROWS[2], 2]).then_inc(pj_free[n], 1)

            def self_exps(i):
                for u in range(PAIR * G):
                    n = filled(act, SC_USES, sc_full, f"self{u}", i)
                    nc.scalar.activation(p_self[:S, u, :], sc[n][:S, :RS], ACT.Exp, scale=SCALE).then_inc(sc_free[n], 1)

            def cross_exps(i, b):
                for u in range(b * TT * G, (b + 1) * TT * G):
                    rows = TROWS[u // G % TT]
                    n = filled(act, SC_USES, sc_full, f"cross{u}", i)
                    nc.scalar.activation(p_cross[:rows, u, :], sc[n][:rows, :RS], ACT.Exp, scale=SCALE).then_inc(sc_free[n], 1)

            def copy_out(before, b, dst):
                act.wait_ge(ot_full[b], before + 1)
                nc.scalar.copy(dst[:, b, :], ot[b][:, :RS]).then_inc(ot_free[b], 1)

            def body(i):
                if on("self", i):
                    copy_kv(i)
                    max_high("self_max", i, ms_parts)
                    self_exps(i)
                    for b in range(PAIR):
                        copy_out(ot_uses("self", i), b, outT_s)
                if on("cross", i):
                    max_high("cross_max", i, mx_parts)
                if on("next", i):
                    copy_T("xT", i, xT)
                    high("q", i, "q", q_parts, i + 1)
                if on("self", i):
                    copy_T("self_t2", i, oT_s)
                if on("next", i):
                    high("k", i, "k", k_parts, i + 1)
                    copy_v(i)
                if on("cross", i):
                    cross_exps(i, 0)
                    copy_out(ot_uses("cross", i - 1), 0, outT_x)
                if on("self", i):
                    copy_T("x1T", i, x1T)
                    high("qx", i, "qx", qx_parts, i)
                if on("cross", i):
                    cross_exps(i, 1)
                    copy_out(ot_uses("cross", i - 1), 1, outT_x)
                if on("self", i):
                    copy_vx(i)
                if on("cross", i):
                    copy_T("cross_t2", i, oT_x)

            act.wait_ge(consts_set, NSETS)
            copy_T("xT", -1, xT)
            high("q", -1, "q", q_parts, 0)
            high("k", -1, "k", k_parts, 0)
            copy_v(-1)
            passes(act, body)

            act.wait_ge(coef_step, COEF_STEPS)
            nc.scalar.activation(coef[:, SINV:COSV + 1, :], coef[:, ANG:COSANG + 1, :], ACT.Sin).then_inc(coef_sin, 1)
            act.wait_ge(coef_step, COEF_STEPS + COEF_LAST)

            def phase(q, f):
                if f == 0:
                    for k in range(KT):
                        act.wait_ge(x3T_full, KT * q + k + 1)
                        nc.scalar.copy(x3T[:, k, :], pj[k][:, :NTOK]).then_inc(x3T_ready, 1)
                act.wait_ge(hid_full, FT * q + f + 1)
                nc.scalar.activation(y_sb[:, f % 4, :], hid[f % 4][:, :NTOK], ACT.Identity, bias=coef[:, BIAS, f:f + 1], scale=0.1).then_inc(y_ready, 1)

            def sine(q, f):
                act.wait_ge(rc_ready, FT * q + f + 1)
                nc.scalar.activation(sin_sb[:, f % 4, :], rc_sb[:, f % 4, :], ACT.Sin).then_inc(sin_ready, 1)

            def relu(q, f):
                act.wait_ge(z_ready, FT * q + f + 1)
                nc.scalar.activation(act_sb[f], z_sb[:, f % 4, :], ACT.Relu, bias=coef_in[:, 0, f:f + 1]).then_inc(act_ready, 1)

            def step(q, f, first):
                phase(q, f)
                if f >= 1 or not first:
                    sine(*((q, f - 1) if f >= 1 else (q - 1, FT - 1)))
                if f >= 2 or not first:
                    relu(*((q, f - 2) if f >= 2 else (q - 1, FT + f - 2)))

            for f in range(FT):
                step(0, f, True)
            with act.Fori(1, NQ) as q:
                for f in range(FT):
                    step(q, f, False)
            sine(NQ - 1, FT - 1)
            relu(NQ - 1, FT - 2)
            relu(NQ - 1, FT - 1)

        @block.vector
        def _(dve):
            def norm_stats(n, src, nb, p):
                for b in range(nb):
                    nc.vector.bn_stats(stats[n][:, b, :], src(b)).then_inc(ln_stats[n], 1)
                for b in range(nb):
                    dve.wait_ge(ln_stats[n], nb * p + b + 1)
                    alone(dve)
                    nc.vector.bn_aggr(moments[n][:, b, :], stats[n][:, b, :]).then_inc(ln_moments[n], 1)

            def norm_rows(n, src, dst, nb, p):
                dve.wait_ge(ln_rstd[n], p + 1)
                dve.wait_ge(ln_moments[n], nb * (p + 1))
                for b in range(nb):
                    nc.vector.tensor_scalar(dst[:, b, :], src(b), moments[n][:, b, 0:1], rstd[n][:, b:b + 1], ALU.subtract, ALU.mult).then_inc(xn_ready[n], 1)

            def rest(step, i, name, parts, dst, p):
                n, before = use(PJ_USES, step, i)
                dve.wait_ge(high_ready[name], p + 1)
                at_least(dve, low_ready[name], p)
                nc.vector.tensor_tensor(dst[:], pj[n][:, :KT * N].rearrange("p (m n) -> p m n", m=KT), parts[:, :, 0, :], ALU.subtract).then_inc(pj_free[n], 1)

            def rest_kv(i):
                for b in range(PAIR):
                    n, before = use(PJ_USES, f"kv{b}", i)
                    dve.wait_ge(high_ready["kx"], PAIR * i + b + 1)
                    at_least(dve, low_ready["kx"], PAIR * i)
                    nc.vector.tensor_tensor(kx_rest[:64, b, :], pj[n][:64, :T], kx_parts[:64, 0, b, :], ALU.subtract).then_inc(pj_free[n], 1)

            def split_maxima(name, i, parts, left, p):
                n, before = use(PJ_USES, name, i)
                dve.wait_ge(high_ready[name], p + 1)
                nc.vector.tensor_tensor(left[:], pj[n][:H * PAIR, :S], parts[:, 0, :], ALU.subtract).then_inc(pj_free[n], 1)
                dve.wait_ge(pj_free[n], before + 1)
                nc.vector.tensor_copy(parts[:, 1, :], left[:]).then_inc(mid_ready[name], 1)
                dve.wait_ge(mid_ready[name], p + 1)
                nc.vector.tensor_tensor(parts[:, 2, :], left[:], parts[:, 1, :], ALU.subtract).then_inc(low_ready[name], 1)

            def self_maxima(i):
                for u in range(PAIR * G):
                    b, g = divmod(u, G)
                    n = filled(dve, MX_USES, mx_full, f"self{u}", i)
                    nc.vector.reduce_max(max_s[:, g * R:(g + 1) * R, b], mx[n][:S, :RS].rearrange("q (r k) -> q r k", r=R), AX.X).then_inc(mx_free[n], 1)

            def cross_maxima(i):
                for u in range(PAIR * H):
                    b, h = divmod(u, H)
                    n = filled(dve, MX_USES, mx_full, f"cross{u}", i)
                    nc.vector.reduce_max(max_x[:, h, b:b + 1], mx[n][:S, :T], AX.X).then_inc(mx_free[n], 1)

            def normalise(kind, i, b, recip, o, p):
                n = filled(dve, PJ_USES, pj_full, f"{kind}_t1_{b}", i)
                heads = pj[n][:S, :].rearrange("s (r g c) -> s r g c", g=G, c=VW)
                nc.vector.reciprocal(recip[:, b, :, :], heads[:, :, :, HD]).then_inc(recip_ready[kind], 1)
                dve.wait_ge(recip_ready[kind], PAIR * p + b + 1)
                nc.vector.tensor_tensor(o[:, b, :].rearrange("s (g r d) -> s r g d", g=G, r=R), heads[:, :, :, :HD],
                                        recip[:, b, :, :].unsqueeze(3).broadcast_to([S, R, G, HD]), ALU.mult).then_inc(pj_free[n], 1)

            def residual(step, i, dst, src):
                n = filled(dve, PJ_USES, pj_full, step, i)
                nc.vector.tensor_tensor(dst[:].rearrange("s b d -> s (b d)"), pj[n][:S, :], src[:].rearrange("s b d -> s (b d)"), ALU.add).then_inc(pj_free[n], 1)

            def first_norm(p):
                dve.wait_ge(xl_in, 16 * (p + 1))
                norm_stats(0, lambda b: xl[:, b, :], PAIR, p)
                norm_rows(0, lambda b: xl[:, b, :], xn1, PAIR, p)

            def body(i):
                if on("self", i):
                    self_maxima(i)
                    rest_kv(i)
                    split_maxima("self_max", i, ms_parts, ms_rest, i)
                if on("next", i):
                    first_norm(i + 1)
                if on("cross", i):
                    cross_maxima(i)
                    split_maxima("cross_max", i, mx_parts, mx_rest, i - 1)
                if on("self", i):
                    for b in range(PAIR):
                        normalise("self", i, b, recip_s, o_s, i)
                if on("next", i):
                    rest("q", i, "q", q_parts, q_rest, i + 1)
                    rest("k", i, "k", k_parts, k_rest, i + 1)
                if on("self", i):
                    dve.wait_ge(xr_in, 16 * (i + 1))
                    at_least(dve, x1r_ready, i)
                    residual("self_o", i, x1, xr)
                    copied(dve, "self_o", i)
                    norm_stats(1, lambda b: x1[:, b, :], PAIR, i)
                    norm_rows(1, lambda b: x1[:, b, :], xn2, PAIR, i)
                    rest("qx", i, "qx", qx_parts, qx_rest, i)
                if on("cross", i):
                    for b in range(PAIR):
                        normalise("cross", i, b, recip_x, o_x, i - 1)
                    dve.wait_ge(x1r_ready, i)
                    dve.wait_ge(x2_kept, 16 * i)
                    residual("cross_o", i, x2, x1r)

            nc.vector.memset(k_stack[KROWS:KM], -1.0)
            nc.vector.memset(kx_stack[KROWS:KM], -1.0)
            dve.wait_ge(first_in, 16 * NFIRST)
            nc.vector.tensor_copy(ident_bf[:], ident_sb[:])
            for r in range(R):
                nc.vector.tensor_copy(mask_bf[:, r, :], mask_f[:, 0, :])
                last = nc.vector.tensor_copy(maskT_bf[:, r, :], mask_f[:, 1, :])
            last.then_inc(masks_set, 1)
            first_norm(0)
            rest("q", -1, "q", q_parts, q_rest, 0)
            rest("k", -1, "k", k_parts, k_rest, 0)

            done = [0]

            def then(ins):
                done[0] += 1
                ins.then_inc(coef_step, 1)
                dve.wait_ge(coef_step, done[0])

            ph, sinr, cosr = coef_in[:, 1, :], coef[:, ANG, :], coef[:, COSANG, :]
            n1, n2 = coef[:, N1, :], coef[:, N2, :]
            dve.wait_ge(coefs_in, 16)
            then(nc.vector.tensor_scalar(n1, ph, INV_TWO_PI, ROUND, ALU.mult, ALU.add))
            then(nc.vector.tensor_scalar(n2, n1, ROUND, None, ALU.subtract))
            then(nc.vector.scalar_tensor_tensor(sinr, n2, -C1, ph, ALU.mult, ALU.add))
            then(nc.vector.scalar_tensor_tensor(cosr, n2, -C2, sinr, ALU.mult, ALU.add))
            then(nc.vector.tensor_scalar(sinr, cosr, PI_BELOW, -PI_BELOW, ALU.min, ALU.max))
            then(nc.vector.tensor_scalar(n1, sinr, float(np.pi / 2), None, ALU.add))
            then(nc.vector.tensor_scalar(n2, n1, INV_TWO_PI, ROUND, ALU.mult, ALU.add))
            then(nc.vector.tensor_scalar(cosr, n2, ROUND, -TWO_PI, ALU.subtract, ALU.mult))
            then(nc.vector.tensor_tensor(n2, cosr, n1, ALU.add))
            then(nc.vector.tensor_scalar(cosr, n2, PI_BELOW, -PI_BELOW, ALU.min, ALU.max))
            assert done[0] == COEF_STEPS
            passes(dve, body)

            dve.wait_ge(coef_sin, 1)
            amp, bias = coef[:, AMP, :], coef[:, BIAS, :]
            then(nc.vector.tensor_tensor(n1, coef[:, COSV, :], coef_in[:, 2, :], ALU.mult))
            then(nc.vector.tensor_tensor(n2, coef[:, SINV, :], coef_in[:, 3, :], ALU.mult))
            then(nc.vector.tensor_tensor(cosr, n1, n2, ALU.add))
            then(nc.vector.scalar_tensor_tensor(amp, cosr, 0.1, coef_in[:, 3, :], ALU.mult, ALU.mult))
            then(nc.vector.scalar_tensor_tensor(bias, coef_in[:, 0, :], 0.1, sinr, ALU.mult, ALU.add))
            assert done[0] == COEF_STEPS + COEF_LAST

            def third_norm(q):
                at_least(dve, x3T_full, KT * q)
                norm_stats(2, lambda b: x2_all[:, bass.ds(QB * q + b, 1), :].rearrange("s o d -> s (o d)"), QB, q)
                norm_rows(2, lambda b: x2_all[:, bass.ds(QB * q + b, 1), :].rearrange("s o d -> s (o d)"), xn3, QB, q)

            def reduce_phase(q, f):
                t, c = FT * q + f + 1, f % 4
                dve.wait_ge(y_ready, t)
                nc.vector.tensor_scalar(n_sb[:, c, :], y_sb[:, c, :], INV_TWO_PI, ROUND, ALU.mult, ALU.add).then_inc(n_ready, 1)
                dve.wait_ge(n_ready, t)
                nc.vector.tensor_scalar(m_sb[:, c, :], n_sb[:, c, :], ROUND, -TWO_PI, ALU.subtract, ALU.mult).then_inc(m_ready, 1)
                dve.wait_ge(m_ready, t)
                nc.vector.tensor_tensor(r_sb[:, c, :], y_sb[:, c, :], m_sb[:, c, :], ALU.add).then_inc(r_ready, 1)
                dve.wait_ge(r_ready, t)
                nc.vector.tensor_scalar(rc_sb[:, c, :], r_sb[:, c, :], PI_BELOW, -PI_BELOW, ALU.min, ALU.max).then_inc(rc_ready, 1)

            def modulate(q, f):
                dve.wait_ge(sin_ready, FT * q + f + 1)
                nc.vector.scalar_tensor_tensor(z_sb[:, f % 4, :], sin_sb[:, f % 4, :], coef[:, AMP, f:f + 1], hid[f % 4][:, :NTOK],
                                               ALU.mult, ALU.add).then_inc(z_ready, 1)

            def finish(q):
                dve.wait_ge(out_done, 16 * 2 * (q + 1))
                dve.wait_ge(x2b_ready, q + 1)
                for half in range(2):
                    dve.wait_ge(acc_full, 2 * q + half + 1)
                    nc.vector.tensor_tensor(fin[:, 2 * half:2 * half + 2].rearrange("s b d -> s (b d)"), ot[half][:S, :],
                                            x2b[:, 2 * half:2 * half + 2].rearrange("s b d -> s (b d)"), ALU.add).then_inc(fin_ready, 1)

            def step(q, f, first, last):
                reduce_phase(q, f)
                if f >= 1 or not first:
                    modulate(*((q, f - 1) if f >= 1 else (q - 1, FT - 1)))
                if f == 2 and not first:
                    finish(q - 1)
                if f == 4 and not last:
                    third_norm(q + 1)

            dve.wait_ge(x2_kept, 16 * (NP + 1))
            third_norm(0)
            for f in range(FT):
                step(0, f, True, False)
            with dve.Fori(1, NQ - 1) as q:
                for f in range(FT):
                    step(q, f, False, False)
            for f in range(FT):
                step(NQ - 1, f, False, True)
            modulate(NQ - 1, FT - 1)
            finish(NQ - 1)

        @block.gpsimd
        def _(pool):
            def set_to(ap, value):
                nc.gpsimd.memset(ap, value).then_inc(consts_set, 1)

            set_to(half_sb[:], -0.5)
            set_to(v_sb[:, :, HD:HD + 1], 1.0)
            set_to(v_sb[:, :, HD + 1:], 0.0)
            set_to(vx_sb[:, :, :, :, HD:HD + 1].rearrange("p b j g c -> p (b j g) c"), 1.0)
            set_to(vx_sb[:, :, :, :, HD + 1:].rearrange("p b j g c -> p (b j g) c"), 0.0)
            pool.wait_ge(consts_set, NSETS)

            def inverse_std(n, nb, p):
                pool.wait_ge(ln_moments[n], nb * (p + 1))
                alone(pool)
                nc.gpsimd.tensor_scalar(vareps[n][:, :nb], moments[n][:, :nb, 1], EPS, None, ALU.add).then_inc(ln_eps[n], 1)
                pool.wait_ge(ln_eps[n], p + 1)
                nc.gpsimd.tensor_tensor(rstd[n][:, :nb], vareps[n][:, :nb], half_sb[:, :nb], ALU.pow).then_inc(ln_rstd[n], 1)

            def mid_low(name, mid, low, left, count):
                nc.gpsimd.tensor_copy(mid, left).then_inc(mid_ready[name], 1)
                pool.wait_ge(mid_ready[name], count)
                nc.gpsimd.tensor_tensor(low, left, mid, ALU.subtract).then_inc(low_ready[name], 1)

            def split_rest(step, i, parts, left, p):
                copied(pool, step, i)
                alone(pool)
                mid_low(step, parts[:, :, 1, :], parts[:, :, 2, :], left[:], p + 1)

            def body(i):
                if on("self", i):
                    for b in range(PAIR):
                        copied(pool, f"kv{b}", i)
                        alone(pool)
                        mid_low("kx", kx_parts[:64, 1, b, :], kx_parts[:64, 2, b, :], kx_rest[:64, b, :], PAIR * i + b + 1)
                if on("next", i):
                    inverse_std(0, PAIR, i + 1)
                    split_rest("q", i, q_parts, q_rest, i + 1)
                    split_rest("k", i, k_parts, k_rest, i + 1)
                if on("self", i):
                    inverse_std(1, PAIR, i)
                    split_rest("qx", i, qx_parts, qx_rest, i)
                if on("cross", i):
                    pass
                if on("self", i):
                    if on("cross", i):
                        copied(pool, "cross_o", i)
                        alone(pool)
                    nc.gpsimd.tensor_copy(x1r[:], x1[:]).then_inc(x1r_ready, 1)

            inverse_std(0, PAIR, 0)
            split_rest("q", -1, q_parts, q_rest, 0)
            split_rest("k", -1, k_parts, k_rest, 0)
            passes(pool, body)

            pool.wait_ge(ffn_weights_in, 16 * NFFN)
            pool.wait_ge(x2_kept, 16 * (NP + 1))

            def feed(q):
                inverse_std(2, QB, q)
                at_least(pool, fin_ready, 2 * q)
                for b in range(QB):
                    last = nc.gpsimd.tensor_tensor(x2b[:, b, :], x2_all[:, bass.ds(QB * q + b, 1), :].rearrange("s o d -> s (o d)"), b2_sb[:], ALU.add)
                last.then_inc(x2b_ready, 1)
            feed(0)
            with pool.Fori(1, NQ) as q:
                feed(q)


def kernel(**inputs):
    import concourse.bacc as _bacc
    from concourse.bass_utils import run_bass_kernel_spmd as _run

    a = {k: np.asarray(v) for k, v in inputs.items()}
    q, k = np.arange(S)[:, None], np.arange(S)[None, :]
    causal = np.where(k > q, np.float32(MASKED), np.float32(0))
    arrays = {
        "x": a["x"],
        "ctxT": a["ctx_1024"].transpose(0, 2, 1),
        "wq": a["L0_attn_Wq"], "wkv": a["L0_attn_Wkv"], "wo": a["L0_attn_Wo"],
        "cwqT": a["L0_xattn_Wq"].T,
        "cwkvT": np.concatenate([a["L0_xattn_Wk"], a["L0_xattn_Wv"]], 0).T,
        "cwoT": a["L0_xattn_Wo"].T,
        "w1": a["L0_ffn_W1"],
        "coefs": np.stack([a[f"L0_ffn_{n}"].reshape(FT, 128).T for n in ("b1", "quantum_phases", "quantum_weights_real", "quantum_weights_imag")], 1),
        "w2": a["L0_ffn_W2"], "b2": a["L0_ffn_b2"],
        "ident": np.eye(128, dtype=np.float32),
        "mask": np.stack([causal, causal.T], 1),
    }
    nc = _bacc.Bacc("TRN2", target_bir_lowering=False, num_devices=1)
    args = []
    for name in arrays:
        arrays[name] = np.ascontiguousarray(arrays[name])
        args.append(nc.dram_tensor(f"{name}_dram", arrays[name].shape, mybir.dt.from_np(arrays[name].dtype), kind="ExternalInput").ap())
    out = nc.dram_tensor("out_dram", (B, S, D), F32, kind="ExternalOutput").ap()
    decoder(nc, *args, out)
    r = _run(nc, [{f"{n}_dram": v for n, v in arrays.items()}], core_ids=[0])
    return r.results[0]["out_dram"]
```

```python
import numpy as np
import concourse.bass as bass
from concourse import mybir
from contextlib import ExitStack

F32 = mybir.dt.float32
BF16 = mybir.dt.bfloat16
ACT = mybir.ActivationFunctionType
ALU = mybir.AluOpType
AX = mybir.AxisListType

B, S, D, H, T, F = 16, 100, 256, 16, 361, 1024
HD = D // H
G = 4
R = H // G
KT = D // 128
PAIR = 2
NP = B // PAIR
N = PAIR * S
NTERM = 6
KROWS = NTERM * HD
KM = KROWS + 2
Q_RUNS = ((0, 3, 0, True), (3, 2, 0, True), (5, 1, 0, False))
K_RUNS = ((0, 3, 0, False), (3, 2, 1, False), (5, 1, 2, False))
TT = (T + 127) // 128
TROWS = [min(128, T - 128 * j) for j in range(TT)]
VW = 32
RS = R * S
SCALE = HD ** -0.5
MASKED = -262144.0
EPS = 1e-5
FT = F // 128
QB = 4
NQ = B // QB
NTOK = QB * S
TWO_PI = float(np.float32(2 * np.pi))
INV_TWO_PI = float(np.float32(1 / (2 * np.pi)))
PI_BELOW = 3.1415925
ROUND = 1.5 * 2.0 ** 23
C1 = 6.28125
C2 = float(2 * np.pi - 6.28125)
COEF_STEPS, COEF_LAST = 10, 5

PJ_USES = [("xT", "next"), ("q", "next"), ("self_t1_0", "self"), ("k", "next"), ("self_t1_1", "self"), ("self_t2", "self"), ("cross_max0", "cross"),
           ("self_o", "self"), ("x1T", "self"), ("cross_t1_0", "cross"), ("qx", "self"), ("cross_max1", "cross"), ("v", "next"),
           ("self_max", "next"), ("vx0", "self"), ("cross_t1_1", "cross"),
           ("vx1", "self"), ("cross_t2", "cross"), ("kv0", "next"), ("cross_o", "cross"), ("kv1", "next")]
MX_USES = [(f"cross{u}", "cross") for u in range(PAIR * H)] + [(f"self{u}", "next") for u in range(PAIR * G)]
SC_USES = [(f"self{u}", "self") for u in range(PAIR * G)] + [(f"cross{u}", "cross") for u in range(PAIR * TT * G)]


ROWS = [("unit0", 0), ("unit1", 2), ("unit2", 2), ("unit3", 2), ("unit4", 2), ("unit5", 2), ("unit6", 2), ("unit7", 2),
        ("self_t1_1", 2), ("self_t2", 1), ("self_o", 2)] + [(f"keys{n}", 1) for n in range(TT * G)] + [("x1T", 1)]
assert sum(n for _, n in ROWS) == PAIR * H


def rows_at(step):
    at = [s for s, _ in ROWS].index(step)
    return sum(n for _, n in ROWS[:at]), ROWS[at][1]


SELF_MAX_UNIT = 6


def active(i):
    return [p for p, on in (("next", i < NP - 1), ("self", 0 <= i < NP), ("cross", i >= 1)) if on]


def uses_by(uses, banks, n, i):
    return sum(len(range(n, sum(part in active(m) for _, part in uses), banks)) for m in range(-1, i))


def use(uses, banks, step, i):
    m = i if isinstance(i, int) else 1
    at = [s for s, part in uses if part in active(m)].index(step)
    n, before = at % banks, uses_by(uses, banks, at % banks, m) + at // banks
    if isinstance(i, int):
        return n, before
    return n, (i - 1) * len(range(n, len(uses), banks)) + before


def decoder(nc, x, ctxT, wq, wkv, wo, cwqT, cwkvT, cwoT, w1, coefs, w2, b2, ident, mask, out):
    ctx = ExitStack()
    with ctx:
        def sb(name, shape, dt=F32):
            return ctx.enter_context(nc.sbuf_tensor(name, shape, dt))

        def sem(name):
            return ctx.enter_context(nc.semaphore(name))

        qs_dram = nc.dram_tensor("qs_dram", [KT, NTERM, 128, N], BF16, kind="Internal").ap()
        ks_dram = nc.dram_tensor("ks_dram", [KT, NTERM, 128, N], BF16, kind="Internal").ap()
        qx_dram = nc.dram_tensor("qx_dram", [KT, NTERM, 128, N], BF16, kind="Internal").ap()
        kx_dram = nc.dram_tensor("kx_dram", [1, NTERM, G * HD, PAIR * T], BF16, kind="Internal").ap()

        ident_sb = sb("ident_sb", [128, 128])
        ident_bf = sb("ident_bf", [128, 128], BF16)
        mask_bf = sb("mask_bf", [S, R, S], BF16)
        maskT_bf = sb("maskT_bf", [S, R, S], BF16)
        mask_f = sb("mask_f", [S, 2, S])
        wq_sb = sb("wq_sb", [128, KT, D])
        wkv_sb = sb("wkv_sb", [128, KT, 2 * D])
        wo_sb = sb("wo_sb", [128, KT, D])
        cwq_sb = sb("cwq_sb", [128, KT, D])
        cwkv_sb = sb("cwkv_sb", [128, KT, 2 * G * HD])
        cwo_sb = sb("cwo_sb", [128, KT, D])
        w1_sb = sb("w1_sb", [128, KT, F])
        w2_sb = sb("w2_sb", [128, FT, D])
        b2_sb = sb("b2_sb", [S, D])
        half_sb = sb("half_sb", [S, QB])

        xl = sb("xl", [S, PAIR, D])
        xr = sb("xr", [S, PAIR, D])
        kept = sb("kept", [S, B, D])
        stats = [sb(f"stats{n}", [S, QB, 6]) for n in range(3)]
        moments = [sb(f"moments{n}", [S, QB, 2]) for n in range(3)]
        vareps = [sb(f"vareps{n}", [S, QB]) for n in range(3)]
        rstd = [sb(f"rstd{n}", [S, QB]) for n in range(3)]
        xn1 = sb("xn1", [S, PAIR, D])
        xn2 = sb("xn2", [S, PAIR, D])
        xT = sb("xT", [128, KT, N])
        x1T = sb("x1T", [128, KT, N])
        ctxT_sb = sb("ctxT_sb", [128, KT, PAIR, T])
        q_parts = sb("q_parts", [128, KT, 3, N], BF16)
        k_parts = sb("k_parts", [128, KT, 3, N], BF16)
        qx_parts = sb("qx_parts", [128, KT, 3, N], BF16)
        kx_parts = sb("kx_parts", [G * HD, 3, PAIR, T], BF16)
        q_rest = sb("q_rest", [128, KT, N])
        k_rest = sb("k_rest", [128, KT, N])
        qx_rest = sb("qx_rest", [128, KT, N])
        kx_rest = sb("kx_rest", [G * HD, PAIR, T])
        q_stack = sb("q_stack", [128, H, N], BF16)
        k_stack = sb("k_stack", [128, H, N], BF16)
        qx_stack = [sb(f"qx_stack{n}", [128, H, N], BF16) for n in range(2)]
        kx_stack = [sb(f"kx_stack{n}", [128, G, PAIR, T], BF16) for n in range(2)]
        vT = sb("vT", [128, PAIR, T])
        v_sb = sb("v_sb", [S, PAIR * H, VW])
        vx_sb = sb("vx_sb", [128, PAIR, TT, G, VW])
        max_s = sb("max_s", [S, H, PAIR])
        max_x = sb("max_x", [S, PAIR, H])
        ms_parts = sb("ms_parts", [H * PAIR, 2, S], BF16)
        mx_parts = sb("mx_parts", [H, PAIR, 2, S], BF16)
        p_self = sb("p_self", [128, PAIR * G, RS])
        p_cross = sb("p_cross", [128, PAIR * TT * G, RS])
        outT_s = sb("outT_s", [128, PAIR, RS])
        outT_x = sb("outT_x", [128, PAIR, RS])
        recip_s = sb("recip_s", [S, PAIR, R, G])
        recip_x = sb("recip_x", [S, PAIR, R, G])
        o_s = sb("o_s", [S, PAIR, D])
        o_x = sb("o_x", [S, PAIR, D])
        oT_s = sb("oT_s", [128, KT, N])
        oT_x = sb("oT_x", [128, KT, N])

        xn3 = qx_stack[0][:S].rearrange("p h n -> p (h n)").bitcast(F32)[:, :QB * D].rearrange("p (b d) -> p b d", d=D)
        x2b = qx_stack[1][:S].rearrange("p h n -> p (h n)").bitcast(F32)[:, :QB * D].rearrange("p (b d) -> p b d", d=D)
        x3T = outT_s
        coef_in = sb("coef_in", [128, 4, FT])
        coef = sb("coef", [128, 8, FT])
        ANG, COSANG, N1, N2, SINV, COSV, AMP, BIAS = range(8)
        y_sb, n_sb, m_sb, r_sb, rc_sb, sin_sb = (p_cross[:, 4 * n:4 * n + 4, :] for n in range(6))
        z_sb = p_self[:, :4, :]
        stack_f32 = q_stack[:].rearrange("p h n -> p (h n)").bitcast(F32).rearrange("p (f n) -> p f n", n=NTOK)
        act_sb = [p_self[:, 4 + f, :] for f in range(4)] + [stack_f32[:, f, :] for f in range(4)]
        fin = k_stack[:S].rearrange("p h n -> p (h n)").bitcast(F32)[:, :QB * D].rearrange("p (b d) -> p b d", d=D)

        mx = [ctx.enter_context(nc.psum_tensor(f"mx{n}", [128, 512], F32)) for n in range(3)]
        sc = [ctx.enter_context(nc.psum_tensor(f"sc{n}", [128, 512], F32)) for n in range(2)]
        ot = ctx.enter_context(nc.psum_tensor("ot", [128, 512], F32))
        pj = [ctx.enter_context(nc.psum_tensor(f"pj{n}", [128, 512], F32)) for n in range(2)]
        hid = [mx[0], mx[1], mx[2], sc[0]]
        acc = [sc[1], ot]

        first_in = sem("first_in")
        attn_weights_in = sem("attn_weights_in")
        ffn_weights_in = sem("ffn_weights_in")
        coefs_in = sem("coefs_in")
        waits_carried = sem("waits_carried")
        consts_set = sem("consts_set")
        masks_set = sem("masks_set")
        xl_in = sem("xl_in")
        xr_in = sem("xr_in")
        ctx_in = sem("ctx_in")
        ln_stats = [sem(f"ln{n}_stats") for n in range(3)]
        ln_moments = [sem(f"ln{n}_moments") for n in range(3)]
        ln_eps = [sem(f"ln{n}_eps") for n in range(3)]
        ln_rstd = [sem(f"ln{n}_rstd") for n in range(3)]
        xn_ready = [sem(f"xn{n}_ready") for n in range(3)]
        pj_full = [sem(f"pj_full{n}") for n in range(2)]
        pj_free = [sem(f"pj_free{n}") for n in range(2)]
        mx_full = [sem(f"mx_full{n}") for n in range(3)]
        mx_free = [sem(f"mx_free{n}") for n in range(3)]
        sc_full = [sem(f"sc_full{n}") for n in range(2)]
        sc_free = [sem(f"sc_free{n}") for n in range(2)]
        ot_full = sem("ot_full")
        ot_free = sem("ot_free")
        split = ("q", "k", "qx", "kx", "self_max", "cross_max")
        high_ready = {n: sem(f"{n}_high") for n in split}
        mid_ready = {n: sem(f"{n}_mid") for n in split}
        low_ready = {n: sem(f"{n}_low") for n in split}
        parts_out = {n: sem(f"{n}_out") for n in split[:4]}
        self_stacks_in = sem("self_stacks_in")
        cross_stacks_in = sem("cross_stacks_in")
        maxima_in = {n: sem(f"{n}_in") for n in split[4:]}
        vT_ready = sem("vT_ready")
        recip_ready = {k: sem(f"{k}_recip") for k in ("self", "cross")}
        coef_step = sem("coef_step")
        coef_sin = sem("coef_sin")
        x3T_full = sem("x3T_full")
        x3T_ready = sem("x3T_ready")
        hid_full = sem("hid_full")
        y_ready = sem("y_ready")
        n_ready = sem("n_ready")
        m_ready = sem("m_ready")
        r_ready = sem("r_ready")
        rc_ready = sem("rc_ready")
        sin_ready = sem("sin_ready")
        z_ready = sem("z_ready")
        act_ready = sem("act_ready")
        acc_full = sem("acc_full")
        fin_ready = sem("fin_ready")
        x2b_ready = sem("x2b_ready")
        out_done = sem("out_done")

        block = ctx.enter_context(nc.Block())
        NSETS = 5
        NFIRST, NATTN, NFFN = 5, 3, 3
        STACKED = 16 * 2
        WRITTEN = 16 * len(Q_RUNS)
        SENT = 16 * 2

        def at_least(eng, s, n):
            if not isinstance(n, int) or n > 0:
                eng.wait_ge(s, n)

        def alone(eng):
            eng.sem_inc(waits_carried, 1)

        def filled(eng, uses, full, step, i):
            n, before = use(uses, len(full), step, i)
            eng.wait_ge(full[n], before + 1)
            return n

        def copied(eng, step, i):
            n, before = use(PJ_USES, 2, step, i)
            eng.wait_ge(pj_free[n], before + 1)

        def on(part, i):
            return not isinstance(i, int) or part in active(i)

        def passes(eng, body):
            body(0, 0)
            with eng.Fori(0, (NP - 2) // 2) as j:
                body(2 * j + 1, 1)
                body(2 * j + 2, 0)
            body(NP - 1, 1)
            body(NP, 0)

        def ot_uses(kind, p, b):
            if kind == "self":
                return b if isinstance(p, int) and p == 0 else 4 * p - 2 + b
            return 4 * p + 2 + b if isinstance(p, int) and p == NP - 1 else 4 * p + 4 + b

        @block.sync
        def _(sp):
            def wait(s, n):
                at_least(sp, s, n)
                alone(sp)

            def wait_copied(step, i):
                copied(sp, step, i)
                alone(sp)

            def rows(b0, n):
                return x[bass.ds(b0, n)].rearrange("b s d -> s b d")

            def load_ctx(p):
                for b in range(PAIR):
                    sp.dma_start(ctxT_sb[:, :, b, :], ctxT[PAIR * p + b].rearrange("(k p) t -> p k t", p=128)
                                 if isinstance(p, int) else
                                 ctxT[bass.ds(PAIR * p + b, 1)].rearrange("o (k p) t -> p (o k) t", p=128)).then_inc(ctx_in, 16)

            def parts_to_dram(name, parts, dram, runs):
                for at, blocks, part, up in runs:
                    for m in range(dram.shape[0]):
                        src = parts[:, m, part:part + blocks, :] if up else parts[:, m, part:part + 1, :].broadcast_to([parts.shape[0], blocks, parts.shape[3]])
                        sp.dma_start(dram[m, at:at + blocks].rearrange("t p s -> p t s"), src).then_inc(parts_out[name], 16)

            def stack(dst, dram, name, p, done):
                wait(parts_out[name], WRITTEN * dram.shape[0] * (p + 1))
                sp.dma_start(dst[:KROWS], dram.rearrange("m t (d h) s -> (t d) m (h s)", d=HD)).then_inc(done, 16)

            def by_tile(stack):
                return stack[:].rearrange("p (m h) s -> p m (h s)", m=KT)

            def body(i, odd):
                if on("next", i) and on("self", i):
                    wait(xn_ready[0], PAIR * (i + 1))
                    sp.dma_start(xl[:], rows(PAIR * (i + 1), PAIR)).then_inc(xl_in, 16)
                if on("self", i):
                    wait(ln_stats[1], PAIR * i)
                    sp.dma_start(xr[:], rows(PAIR * i, PAIR)).then_inc(xr_in, 16)
                if on("self", i):
                    wait(low_ready["kx"], PAIR * (i + 1))
                    wait(cross_stacks_in, STACKED * i)
                    parts_to_dram("kx", kx_parts[:G * HD].rearrange("p t b n -> p t (b n)").unsqueeze(1), kx_dram, K_RUNS)
                    if on("next", i):
                        load_ctx(i + 1)
                if on("next", i):
                    wait(low_ready["q"], i + 2)
                    parts_to_dram("q", q_parts, qs_dram, Q_RUNS)
                if on("cross", i):
                    send_cross_maxima(i, 0, qx_stack[1 - odd])
                if on("next", i):
                    wait(low_ready["k"], i + 2)
                    parts_to_dram("k", k_parts, ks_dram, K_RUNS)
                    if on("self", i):
                        wait(ot_free, ot_uses("self", i, 1) + 1)
                    stack(by_tile(q_stack), qs_dram, "q", i + 1, self_stacks_in)
                    stack(by_tile(k_stack), ks_dram, "k", i + 1, self_stacks_in)
                if on("cross", i):
                    send_cross_maxima(i, 1, qx_stack[1 - odd])
                if on("self", i):
                    wait(low_ready["qx"], i + 1)
                    parts_to_dram("qx", qx_parts, qx_dram, Q_RUNS)
                    stack(by_tile(qx_stack[odd]), qx_dram, "qx", i, cross_stacks_in)
                    stack(kx_stack[odd][:].rearrange("p g b n -> p (g b n)").unsqueeze(1), kx_dram, "kx", i, cross_stacks_in)

                if on("next", i):
                    wait(high_ready["self_max"], i + 2)
                    send_maxima("self_max", "self_max", i, q_stack, slice(0, N), ms_parts[:])

            def send_cross_maxima(i, b, dst):
                wait(high_ready["cross_max"], PAIR * (i - 1) + b + 1)
                send_maxima("cross_max", f"cross_max{b}", i, dst, slice(b * S, (b + 1) * S), mx_parts[:, b])

            def send_maxima(name, step, i, dst, tokens, parts):
                for t in range(2):
                    if t == 1:
                        wait_copied(step, i)
                    sp.dma_start(dst[KROWS + t:KROWS + t + 1, :, tokens], parts[:, t, :]).then_inc(maxima_in[name], 16)

            def weights(pairs, done):
                for dst, src in pairs:
                    sp.dma_start(dst[:], src.rearrange("(k p) n -> p k n", p=128)).then_inc(done, 16)

            sp.sem_inc(out_done, 16 * 2)
            sp.dma_start(xl[:], rows(0, PAIR)).then_inc(xl_in, 16)
            sp.dma_start(ident_sb[:], ident).then_inc(first_in, 16)
            sp.dma_start(mask_f[:], mask).then_inc(first_in, 16)
            weights(((wq_sb, wq), (wkv_sb, wkv), (cwkv_sb, cwkvT)), first_in)
            load_ctx(0)
            weights(((wo_sb, wo), (cwq_sb, cwqT), (cwo_sb, cwoT)), attn_weights_in)
            body(-1, 1)
            weights(((w1_sb, w1), (w2_sb, w2)), ffn_weights_in)
            sp.dma_start(b2_sb[:], b2.partition_broadcast(S)).then_inc(ffn_weights_in, 16)
            sp.dma_start(coef_in[:], coefs).then_inc(coefs_in, 16)
            passes(sp, body)

            def store(q):
                for half in range(2):
                    wait(fin_ready, 2 * q + half + 1)
                    sp.dma_start(out[bass.ds(QB * q + 2 * half, 2)].rearrange("b s d -> s b d"), fin[:, 2 * half:2 * half + 2]).then_inc(out_done, 16)
            with sp.Fori(0, NQ) as q:
                store(q)
            wait(out_done, 16 * 2 * (NQ + 1))

        @block.tensor
        def _(pe):
            def bank(step, i):
                n, before = use(PJ_USES, 2, step, i)
                at_least(pe, pj_free[n], before)
                return pj[n], pj_full[n]

            def transpose_rows(step, i, src):
                into, full = bank(step, i)
                for k in range(KT):
                    for b in range(PAIR):
                        last = nc.tensor.transpose(into[:, k * N + b * S:k * N + (b + 1) * S], src[:, b, k * 128:(k + 1) * 128], ident_sb[:S, :S])
                last.then_inc(full, 1)

            def project_T(step, i, w, srcT, read_step):
                into, full = bank(step, i)
                copied(pe, read_step, i)
                for m in range(KT):
                    for k in range(KT):
                        last = nc.tensor.matmul(into[:, m * N:(m + 1) * N], w[:, k, m * 128:(m + 1) * 128], srcT[:, k, :], start=(k == 0), stop=(k == KT - 1))
                last.then_inc(full, 1)

            def project_rows(step, i, w, srcT, read_step):
                into, full = bank(step, i)
                copied(pe, read_step, i)
                for b in range(PAIR):
                    for k in range(KT):
                        last = nc.tensor.matmul(into[:S, b * D:(b + 1) * D], srcT[:, k, b * S:(b + 1) * S], w[:, k, :], start=(k == 0), stop=(k == KT - 1))
                last.then_inc(full, 1)

            def kv_cross(i, b):
                pe.wait_ge(ctx_in, 16 * PAIR * (i + 2))
                into, full = bank(f"kv{b}", i)
                for k in range(KT):
                    last = nc.tensor.matmul(into[:, :T], cwkv_sb[:, k, :], ctxT_sb[:, k, b, :], start=(k == 0), stop=(k == KT - 1))
                last.then_inc(full, 1)

            def v_cross(i, b):
                pe.wait_ge(vT_ready, PAIR * i + b + 1)
                into, full = bank(f"vx{b}", i)
                alone(pe)
                for j in range(TT):
                    last = nc.tensor.transpose(into[:TROWS[j], j * 64:(j + 1) * 64], vT[64:, b, j * 128:j * 128 + TROWS[j]], ident_sb[64:, 64:])
                last.then_inc(full, 1)

            def self_rows(i, first, count):
                if not on("next", i):
                    return
                if first == 0:
                    pe.wait_ge(self_stacks_in, STACKED * (i + 2))
                for u in range(first, first + count):
                    b, g = divmod(u, G)
                    n, before = use(MX_USES, 3, f"self{u}", i)
                    at_least(pe, mx_free[n], before)
                    nc.tensor.matmul(mx[n][:S, :RS], ident_bf[:S, :S], mask_bf[:].rearrange("q h k -> q (h k)"), start=True, stop=False, skip_group_check=True)
                    for r in range(R):
                        h = g * R + r
                        last = nc.tensor.matmul(mx[n][:S, r * S:(r + 1) * S], q_stack[:KROWS, h, b * S:(b + 1) * S],
                                                k_stack[:KROWS, h, b * S:(b + 1) * S], start=False, stop=(r == R - 1), skip_group_check=True)
                    last.then_inc(mx_full[n], 1)

            def cross_rows(i, odd, *steps):
                if not on("cross", i):
                    return
                for u in (u for step in steps for u in range(rows_at(step)[0], sum(rows_at(step)))):
                    if u == 0:
                        pe.wait_ge(cross_stacks_in, STACKED * i)
                    b, h = divmod(u, H)
                    n, before = use(MX_USES, 3, f"cross{u}", i)
                    at_least(pe, mx_free[n], before)
                    nc.tensor.matmul(mx[n][:S, :T], qx_stack[1 - odd][:KROWS, h, b * S:(b + 1) * S], kx_stack[1 - odd][:KROWS, h // R, b, :],
                                     start=True, stop=True).then_inc(mx_full[n], 1)

            def maxima_T(step, i, src, last_unit):
                into, full = bank(step, i)
                n, before = use(MX_USES, 3, last_unit, i)
                pe.wait_ge(mx_free[n], before + 1)
                nc.tensor.transpose(into[:src.shape[1], :S], src, ident_sb[:S, :S]).then_inc(full, 1)

            def self_keys(i, between):
                pe.wait_ge(maxima_in["self_max"], SENT * (i + 1))

                def scores(u):
                    b, g = divmod(u, G)
                    n, before = use(SC_USES, 2, f"self{u}", i)
                    at_least(pe, sc_free[n], before)
                    nc.tensor.matmul(sc[n][:S, :RS], ident_bf[:S, :S], maskT_bf[:].rearrange("k h q -> k (h q)"), start=True, stop=False, skip_group_check=True)
                    for r in range(R):
                        h = g * R + r
                        last = nc.tensor.matmul(sc[n][:S, r * S:(r + 1) * S], k_stack[:KM, h, b * S:(b + 1) * S],
                                                q_stack[:KM, h, b * S:(b + 1) * S], start=False, stop=(r == R - 1), skip_group_check=True)
                    last.then_inc(sc_full[n], 1)

                def values(u):
                    b, g = divmod(u, G)
                    n, before = use(SC_USES, 2, f"self{u}", i)
                    pe.wait_ge(sc_free[n], before + 1)
                    if g == 0:
                        at_least(pe, ot_free, ot_uses("self", i, b))
                    for r in range(R):
                        last = nc.tensor.matmul(ot[g * VW:(g + 1) * VW, r * S:(r + 1) * S], v_sb[:, b * H + g * R + r, :],
                                                p_self[:S, u, r * S:(r + 1) * S], start=True, stop=True)
                    if g == G - 1:
                        last.then_inc(ot_full, 1)

                for u in range(PAIR * G + 1):
                    if u < PAIR * G:
                        scores(u)
                        between(u)
                    if u >= 1:
                        values(u - 1)

            def cross_keys(i, odd, b, between):
                pe.wait_ge(maxima_in["cross_max"], SENT * (PAIR * (i - 1) + b + 1))

                def scores(j, g):
                    n, before = use(SC_USES, 2, f"cross{(b * TT + j) * G + g}", i)
                    at_least(pe, sc_free[n], before)
                    nc.tensor.matmul(sc[n][:TROWS[j], :RS].rearrange("p (r s) -> p r s", r=R), kx_stack[1 - odd][:KM, g, b, j * 128:j * 128 + TROWS[j]],
                                     qx_stack[1 - odd][:KM, g * R:(g + 1) * R, b * S:(b + 1) * S], start=True, stop=True).then_inc(sc_full[n], 1)

                def values(j, g):
                    u = (b * TT + j) * G + g
                    n, before = use(SC_USES, 2, f"cross{u}", i)
                    pe.wait_ge(sc_free[n], before + 1)
                    last = nc.tensor.matmul(ot[g * VW:(g + 1) * VW, :RS], vx_sb[:TROWS[j], b, j, g, :], p_cross[:TROWS[j], u, :],
                                            start=(j == 0), stop=(j == TT - 1))
                    if j == TT - 1 and g == G - 1:
                        last.then_inc(ot_full, 1)

                units = [(j, g) for j in range(TT) for g in range(G)]
                for n, (j, g) in enumerate(units):
                    scores(j, g)
                    between(n)
                    if n % G == 1 and n > G:
                        if n == G + 1:
                            pe.wait_ge(ot_free, ot_uses("cross", i - 1, b))
                        for m in range(n - 1 - G, n - 1):
                            values(*units[m])
                for m in range(len(units) - G, len(units)):
                    values(*units[m])

            def heads_to_rows(kind, i, b, outT, p):
                into, full = bank(f"{kind}_t1_{b}", i)
                pe.wait_ge(ot_free, ot_uses(kind, p, b) + 1)
                for r in range(R):
                    last = nc.tensor.transpose(into[:S, r * 128:(r + 1) * 128], outT[:, b, r * S:(r + 1) * S], ident_sb[:])
                last.then_inc(full, 1)

            def body(i, odd):
                def first_steps(u):
                    if on("next", i) and u == 5:
                        pe.wait_ge(xn_ready[0], PAIR * (i + 2))
                        transpose_rows("xT", i, xn1)
                    if on("next", i) and u == 5:
                        project_T("q", i, wq_sb, xT, "xT")
                    if on("self", i) and u == 6:
                        heads_to_rows("self", i, 0, outT_s, i)
                    if on("next", i) and u == 7:
                        project_T("k", i, wkv_sb, xT, "xT")
                    cross_rows(i, odd, f"unit{u}")

                if on("self", i):
                    self_keys(i, first_steps)
                else:
                    for u in range(PAIR * G):
                        first_steps(u)
                if on("self", i):
                    heads_to_rows("self", i, 1, outT_s, i)
                cross_rows(i, odd, "self_t1_1")
                if on("self", i):
                    for b in range(PAIR):
                        copied(pe, f"self_t1_{b}", i)
                    transpose_rows("self_t2", i, o_s)
                if on("cross", i):
                    maxima_T("cross_max0", i, max_x[:, 0, :], f"cross{H - 1}")
                cross_rows(i, odd, "self_t2")
                if on("self", i):
                    project_rows("self_o", i, wo_sb, oT_s, "self_t2")
                cross_rows(i, odd, "self_o")
                if on("cross", i):
                    cross_keys(i, odd, 0, lambda n: cross_rows(i, odd, f"keys{n}"))
                if on("self", i):
                    pe.wait_ge(xn_ready[1], PAIR * (i + 1))
                    transpose_rows("x1T", i, xn2)
                cross_rows(i, odd, "x1T")
                if on("cross", i):
                    heads_to_rows("cross", i, 0, outT_x, i - 1)
                if on("self", i):
                    project_T("qx", i, cwq_sb, x1T, "x1T")
                if on("cross", i):
                    maxima_T("cross_max1", i, max_x[:, 1, :], f"cross{2 * H - 1}")
                if on("next", i):
                    project_rows("v", i, wkv_sb[:, :, D:], xT, "xT")
                self_rows(i, 0, PAIR * G - SELF_MAX_UNIT)

                def self_maxima(n):
                    if n < SELF_MAX_UNIT:
                        self_rows(i, PAIR * G - SELF_MAX_UNIT + n, 1)
                    if on("next", i) and n == SELF_MAX_UNIT:
                        maxima_T("self_max", i, max_s[:].rearrange("s h b -> s (h b)"), f"self{PAIR * G - 1}")

                if on("cross", i):
                    cross_keys(i, odd, 1, self_maxima)
                else:
                    for n in range(SELF_MAX_UNIT + 1):
                        self_maxima(n)
                if on("self", i):
                    v_cross(i, 0)
                if on("cross", i):
                    heads_to_rows("cross", i, 1, outT_x, i - 1)
                if on("self", i):
                    v_cross(i, 1)
                if on("cross", i):
                    for b in range(PAIR):
                        copied(pe, f"cross_t1_{b}", i)
                    transpose_rows("cross_t2", i, o_x)
                if on("next", i):
                    kv_cross(i, 0)
                if on("cross", i):
                    project_rows("cross_o", i, cwo_sb, oT_x, "cross_t2")
                if on("next", i):
                    kv_cross(i, 1)

            pe.wait_ge(first_in, 16 * NFIRST)
            pe.wait_ge(consts_set, NSETS)
            pe.wait_ge(masks_set, 1)
            body(-1, 1)
            pe.wait_ge(attn_weights_in, 16 * NATTN)
            passes(pe, body)

            pe.wait_ge(ffn_weights_in, 16 * NFFN)
            for uses, free in ((MX_USES, mx_free), (SC_USES, sc_free), (PJ_USES, pj_free)):
                for n in range(len(free)):
                    pe.wait_ge(free[n], uses_by(uses, len(free), n, NP + 1))
            pe.wait_ge(ot_free, 2 * PAIR * NP)

            def hidden(q, f):
                if f == 0:
                    pe.wait_ge(xn_ready[2], QB * (q + 1))
                    for k in range(KT):
                        for b in range(QB):
                            last = nc.tensor.transpose(pj[k][:, b * S:(b + 1) * S], xn3[:, b, k * 128:(k + 1) * 128], ident_sb[:S, :S])
                        last.then_inc(x3T_full, 1)
                    pe.wait_ge(x3T_ready, KT * (q + 1))
                at_least(pe, z_ready, FT * q + f - 3)
                for k in range(KT):
                    last = nc.tensor.matmul(hid[f % 4][:, :NTOK], w1_sb[:, k, f * 128:(f + 1) * 128], x3T[:, k, :], start=(k == 0), stop=(k == KT - 1))
                last.then_inc(hid_full, 1)

            def output(q, f):
                pe.wait_ge(act_ready, FT * q + f + 1)
                if f == 0:
                    at_least(pe, fin_ready, 2 * q)
                for b in range(QB):
                    last = nc.tensor.matmul(acc[b // 2][:S, (b % 2) * D:(b % 2 + 1) * D], act_sb[f][:, b * S:(b + 1) * S], w2_sb[:, f, :],
                                            start=(f == 0 and b % 2 == 0), stop=(f == FT - 1 and b % 2 == 1), skip_group_check=True)
                    if f == FT - 1 and b % 2 == 1:
                        last.then_inc(acc_full, 1)

            LAG = 3
            for f in range(FT):
                hidden(0, f)
                if f >= LAG:
                    output(0, f - LAG)
            with pe.Fori(1, NQ) as q:
                for f in range(FT):
                    hidden(q, f)
                    if f >= LAG:
                        output(q, f - LAG)
                    else:
                        output(q - 1, FT + f - LAG)
            for f in range(FT - LAG, FT):
                output(NQ - 1, f)

        @block.scalar
        def _(act):
            def copy_T(step, i, dst):
                n = filled(act, PJ_USES, pj_full, step, i)
                nc.scalar.copy(dst[:].rearrange("p k n -> p (k n)"), pj[n][:, :KT * N]).then_inc(pj_free[n], 1)

            def high(step, i, name, parts, p):
                n = filled(act, PJ_USES, pj_full, step, i)
                at_least(act, parts_out[name], WRITTEN * KT * p)
                nc.scalar.copy(parts[:, :, 0, :], pj[n][:, :KT * N].rearrange("p (m n) -> p m n", m=KT)).then_inc(high_ready[name], 1)

            def max_high(name, step, i, part):
                n = filled(act, PJ_USES, pj_full, step, i)
                nc.scalar.copy(part, pj[n][:part.shape[0], :S]).then_inc(high_ready[name], 1)

            def copy_v(i):
                n = filled(act, PJ_USES, pj_full, "v", i)
                nc.scalar.copy(v_sb[:, :, :HD], pj[n][:S, :].rearrange("s (h d) -> s h d", d=HD)).then_inc(pj_free[n], 1)

            def copy_kv(i, b):
                if b == 0:
                    at_least(act, parts_out["kx"], WRITTEN * (i + 1))
                n = filled(act, PJ_USES, pj_full, f"kv{b}", i)
                nc.scalar.copy(vT[64:, b, :], pj[n][64:, :T]).then_inc(vT_ready, 1)
                nc.scalar.copy(kx_parts[:64, 0, b, :], pj[n][:64, :T]).then_inc(high_ready["kx"], 1)

            def copy_vx(i, b):
                n = filled(act, PJ_USES, pj_full, f"vx{b}", i)
                v = pj[n][:, :TT * 64].rearrange("t (j g d) -> t j g d", g=G, d=HD)
                nc.scalar.copy(vx_sb[:, b, 0, :, :HD], v[:, 0])
                nc.scalar.copy(vx_sb[:, b, 1, :, :HD], v[:, 1])
                nc.scalar.copy(vx_sb[:TROWS[2], b, 2, :, :HD], v[:TROWS[2], 2]).then_inc(pj_free[n], 1)

            def self_exps(i, first, last):
                for u in range(first, last):
                    n = filled(act, SC_USES, sc_full, f"self{u}", i)
                    nc.scalar.activation(p_self[:S, u, :], sc[n][:S, :RS], ACT.Exp, scale=SCALE).then_inc(sc_free[n], 1)

            def cross_exps(i, b, first, last):
                for u in range(b * TT * G + first, b * TT * G + last):
                    rows = TROWS[u // G % TT]
                    n = filled(act, SC_USES, sc_full, f"cross{u}", i)
                    nc.scalar.activation(p_cross[:rows, u, :], sc[n][:rows, :RS], ACT.Exp, scale=SCALE).then_inc(sc_free[n], 1)

            def copy_out(kind, p, b, dst):
                act.wait_ge(ot_full, ot_uses(kind, p, b) + 1)
                nc.scalar.copy(dst[:, b, :], ot[:, :RS]).then_inc(ot_free, 1)

            def body(i, odd):
                for u in range(PAIR * G):
                    if on("self", i):
                        self_exps(i, u, u + 1)
                    if on("next", i) and u == 5:
                        copy_T("xT", i, xT)
                    if on("next", i) and u == 5:
                        high("q", i, "q", q_parts, i + 1)
                    if on("self", i) and u == G:
                        copy_out("self", i, 0, outT_s)
                    if on("next", i) and u == 7:
                        high("k", i, "k", k_parts, i + 1)
                if on("self", i):
                    copy_out("self", i, 1, outT_s)
                if on("self", i):
                    copy_T("self_t2", i, oT_s)
                if on("cross", i):
                    max_high("cross_max", "cross_max0", i, mx_parts[:, 0, 0, :])
                if on("cross", i):
                    cross_exps(i, 0, 0, TT * G)
                    copy_out("cross", i - 1, 0, outT_x)
                if on("self", i):
                    copy_T("x1T", i, x1T)
                    high("qx", i, "qx", qx_parts, i)
                if on("cross", i):
                    max_high("cross_max", "cross_max1", i, mx_parts[:, 1, 0, :])
                if on("next", i):
                    copy_v(i)
                if on("cross", i):
                    cross_exps(i, 1, 0, SELF_MAX_UNIT + 1)
                if on("next", i):
                    max_high("self_max", "self_max", i, ms_parts[:, 0, :])
                if on("cross", i):
                    cross_exps(i, 1, SELF_MAX_UNIT + 1, TT * G)
                    copy_out("cross", i - 1, 1, outT_x)
                if on("self", i):
                    copy_vx(i, 0)
                    copy_vx(i, 1)
                if on("cross", i):
                    copy_T("cross_t2", i, oT_x)
                if on("next", i):
                    copy_kv(i, 0)
                    copy_kv(i, 1)

            act.wait_ge(consts_set, NSETS)
            body(-1, 1)
            passes(act, body)

            act.wait_ge(coef_step, COEF_STEPS)
            nc.scalar.activation(coef[:, SINV:COSV + 1, :], coef[:, ANG:COSANG + 1, :], ACT.Sin).then_inc(coef_sin, 1)
            act.wait_ge(coef_step, COEF_STEPS + COEF_LAST)

            def phase(q, f):
                if f == 0:
                    for k in range(KT):
                        act.wait_ge(x3T_full, KT * q + k + 1)
                        nc.scalar.copy(x3T[:, k, :], pj[k][:, :NTOK]).then_inc(x3T_ready, 1)
                act.wait_ge(hid_full, FT * q + f + 1)
                nc.scalar.activation(y_sb[:, f % 4, :], hid[f % 4][:, :NTOK], ACT.Identity, bias=coef[:, BIAS, f:f + 1], scale=0.1).then_inc(y_ready, 1)

            def sine(q, f):
                act.wait_ge(rc_ready, FT * q + f + 1)
                nc.scalar.activation(sin_sb[:, f % 4, :], rc_sb[:, f % 4, :], ACT.Sin).then_inc(sin_ready, 1)

            def relu(q, f):
                act.wait_ge(z_ready, FT * q + f + 1)
                nc.scalar.activation(act_sb[f], z_sb[:, f % 4, :], ACT.Relu, bias=coef_in[:, 0, f:f + 1]).then_inc(act_ready, 1)

            def step(q, f, first):
                phase(q, f)
                if f >= 1 or not first:
                    sine(*((q, f - 1) if f >= 1 else (q - 1, FT - 1)))
                if f >= 2 or not first:
                    relu(*((q, f - 2) if f >= 2 else (q - 1, FT + f - 2)))

            for f in range(FT):
                step(0, f, True)
            with act.Fori(1, NQ) as q:
                for f in range(FT):
                    step(q, f, False)
            sine(NQ - 1, FT - 1)
            relu(NQ - 1, FT - 2)
            relu(NQ - 1, FT - 1)

        @block.vector
        def _(dve):
            def batch(b):
                return kept[:, b, :] if isinstance(b, int) else kept[:, bass.ds(b, 1), :].rearrange("s o d -> s (o d)")

            def norm_stats(n, src, nb, p):
                for b in range(nb):
                    nc.vector.bn_stats(stats[n][:, b, :], src(b)).then_inc(ln_stats[n], 1)
                for b in range(nb):
                    dve.wait_ge(ln_stats[n], nb * p + b + 1)
                    alone(dve)
                    nc.vector.bn_aggr(moments[n][:, b, :], stats[n][:, b, :]).then_inc(ln_moments[n], 1)

            def norm_rows(n, src, dst, nb, p):
                dve.wait_ge(ln_rstd[n], p + 1)
                dve.wait_ge(ln_moments[n], nb * (p + 1))
                for b in range(nb):
                    nc.vector.tensor_scalar(dst[:, b, :], src(b), moments[n][:, b, 0:1], rstd[n][:, b:b + 1], ALU.subtract, ALU.mult).then_inc(xn_ready[n], 1)

            def rest(step, i, name, parts, dst, p):
                n, before = use(PJ_USES, 2, step, i)
                dve.wait_ge(high_ready[name], p + 1)
                at_least(dve, low_ready[name], p)
                nc.vector.tensor_tensor(dst[:], pj[n][:, :KT * N].rearrange("p (m n) -> p m n", m=KT), parts[:, :, 0, :], ALU.subtract).then_inc(pj_free[n], 1)

            def rest_kv(i, b):
                n, before = use(PJ_USES, 2, f"kv{b}", i)
                dve.wait_ge(high_ready["kx"], PAIR * (i + 1) + b + 1)
                at_least(dve, low_ready["kx"], PAIR * (i + 1))
                nc.vector.tensor_tensor(kx_rest[:64, b, :], pj[n][:64, :T], kx_parts[:64, 0, b, :], ALU.subtract).then_inc(pj_free[n], 1)

            def second_part(name, step, i, parts, made):
                n, before = use(PJ_USES, 2, step, i)
                dve.wait_ge(high_ready[name], made)
                nc.vector.tensor_tensor(parts[:, 1, :], pj[n][:parts.shape[0], :S], parts[:, 0, :], ALU.subtract).then_inc(pj_free[n], 1)

            def self_maxima(i):
                for u in range(PAIR * G):
                    b, g = divmod(u, G)
                    n = filled(dve, MX_USES, mx_full, f"self{u}", i)
                    nc.vector.reduce_max(max_s[:, g * R:(g + 1) * R, b], mx[n][:S, :RS].rearrange("q (r k) -> q r k", r=R), AX.X).then_inc(mx_free[n], 1)

            def cross_maxima(i, *steps):
                for u in (u for step in steps for u in range(rows_at(step)[0], sum(rows_at(step)))) if on("cross", i) else ():
                    b, h = divmod(u, H)
                    n = filled(dve, MX_USES, mx_full, f"cross{u}", i)
                    nc.vector.reduce_max(max_x[:, b, h:h + 1], mx[n][:S, :T], AX.X).then_inc(mx_free[n], 1)

            def normalise(kind, i, b, recip, o, p):
                n = filled(dve, PJ_USES, pj_full, f"{kind}_t1_{b}", i)
                heads = pj[n][:S, :].rearrange("s (r g c) -> s r g c", g=G, c=VW)
                nc.vector.reciprocal(recip[:, b, :, :], heads[:, :, :, HD]).then_inc(recip_ready[kind], 1)
                dve.wait_ge(recip_ready[kind], PAIR * p + b + 1)
                nc.vector.tensor_tensor(o[:, b, :].rearrange("s (g r d) -> s r g d", g=G, r=R), heads[:, :, :, :HD],
                                        recip[:, b, :, :].unsqueeze(3).broadcast_to([S, R, G, HD]), ALU.mult).then_inc(pj_free[n], 1)

            def residual(step, i, p, src):
                n = filled(dve, PJ_USES, pj_full, step, i)
                nc.vector.tensor_tensor(kept[:, bass.ds(PAIR * p, PAIR), :].rearrange("s b d -> s (b d)"), pj[n][:S, :], src.rearrange("s b d -> s (b d)"),
                                        ALU.add).then_inc(pj_free[n], 1)

            x_of = lambda b: xl[:, b, :]

            def x1_of(i):
                return lambda b: batch(PAIR * i + b)

            def body(i, odd):
                if on("next", i):
                    dve.wait_ge(xl_in, 16 * (i + 2))
                    norm_stats(0, x_of, PAIR, i + 1)
                for u in range(PAIR * G):
                    if on("next", i) and u == 2:
                        norm_rows(0, x_of, xn1, PAIR, i + 1)
                    if on("next", i) and u == 5:
                        rest("q", i, "q", q_parts, q_rest, i + 1)
                    if on("self", i) and u == 6:
                        normalise("self", i, 0, recip_s, o_s, i)
                    if on("next", i) and u == 7:
                        rest("k", i, "k", k_parts, k_rest, i + 1)
                    cross_maxima(i, f"unit{u}")
                if on("self", i):
                    normalise("self", i, 1, recip_s, o_s, i)
                cross_maxima(i, "self_t1_1")
                if on("cross", i):
                    second_part("cross_max", "cross_max0", i, mx_parts[:, 0], PAIR * (i - 1) + 1)
                cross_maxima(i, "self_t2")
                if on("self", i):
                    dve.wait_ge(xr_in, 16 * (i + 1))
                    residual("self_o", i, i, xr[:])
                cross_maxima(i, "self_o")
                if on("self", i):
                    copied(dve, "self_o", i)
                    alone(dve)
                    norm_stats(1, x1_of(i), PAIR, i)
                cross_maxima(i, *(f"keys{n}" for n in range(4)))
                if on("self", i):
                    norm_rows(1, x1_of(i), xn2, PAIR, i)
                cross_maxima(i, *(f"keys{n}" for n in range(4, TT * G)))
                cross_maxima(i, "x1T")
                if on("cross", i):
                    normalise("cross", i, 0, recip_x, o_x, i - 1)
                if on("self", i):
                    rest("qx", i, "qx", qx_parts, qx_rest, i)
                if on("cross", i):
                    second_part("cross_max", "cross_max1", i, mx_parts[:, 1], PAIR * (i - 1) + 2)
                if on("next", i):
                    self_maxima(i)
                    second_part("self_max", "self_max", i, ms_parts[:], i + 2)
                if on("cross", i):
                    normalise("cross", i, 1, recip_x, o_x, i - 1)
                if on("next", i):
                    rest_kv(i, 0)
                if on("cross", i):
                    residual("cross_o", i, i - 1, kept[:, bass.ds(PAIR * (i - 1), PAIR), :])
                if on("next", i):
                    rest_kv(i, 1)

            nc.vector.memset(k_stack[KROWS:KM], -1.0)
            for stack in kx_stack:
                nc.vector.memset(stack[KROWS:KM], -1.0)
            dve.wait_ge(first_in, 16 * NFIRST)
            nc.vector.tensor_copy(ident_bf[:], ident_sb[:])
            for r in range(R):
                nc.vector.tensor_copy(mask_bf[:, r, :], mask_f[:, 0, :])
                last = nc.vector.tensor_copy(maskT_bf[:, r, :], mask_f[:, 1, :])
            last.then_inc(masks_set, 1)
            body(-1, 1)

            done = [0]

            def then(ins):
                done[0] += 1
                ins.then_inc(coef_step, 1)
                dve.wait_ge(coef_step, done[0])

            ph, sinr, cosr = coef_in[:, 1, :], coef[:, ANG, :], coef[:, COSANG, :]
            n1, n2 = coef[:, N1, :], coef[:, N2, :]
            dve.wait_ge(coefs_in, 16)
            then(nc.vector.tensor_scalar(n1, ph, INV_TWO_PI, ROUND, ALU.mult, ALU.add))
            then(nc.vector.tensor_scalar(n2, n1, ROUND, None, ALU.subtract))
            then(nc.vector.scalar_tensor_tensor(sinr, n2, -C1, ph, ALU.mult, ALU.add))
            then(nc.vector.scalar_tensor_tensor(cosr, n2, -C2, sinr, ALU.mult, ALU.add))
            then(nc.vector.tensor_scalar(sinr, cosr, PI_BELOW, -PI_BELOW, ALU.min, ALU.max))
            then(nc.vector.tensor_scalar(n1, sinr, float(np.pi / 2), None, ALU.add))
            then(nc.vector.tensor_scalar(n2, n1, INV_TWO_PI, ROUND, ALU.mult, ALU.add))
            then(nc.vector.tensor_scalar(cosr, n2, ROUND, -TWO_PI, ALU.subtract, ALU.mult))
            then(nc.vector.tensor_tensor(n2, cosr, n1, ALU.add))
            then(nc.vector.tensor_scalar(cosr, n2, PI_BELOW, -PI_BELOW, ALU.min, ALU.max))
            assert done[0] == COEF_STEPS
            passes(dve, body)

            dve.wait_ge(coef_sin, 1)
            amp, bias = coef[:, AMP, :], coef[:, BIAS, :]
            then(nc.vector.tensor_tensor(n1, coef[:, COSV, :], coef_in[:, 2, :], ALU.mult))
            then(nc.vector.tensor_tensor(n2, coef[:, SINV, :], coef_in[:, 3, :], ALU.mult))
            then(nc.vector.tensor_tensor(cosr, n1, n2, ALU.add))
            then(nc.vector.scalar_tensor_tensor(amp, cosr, 0.1, coef_in[:, 3, :], ALU.mult, ALU.mult))
            then(nc.vector.scalar_tensor_tensor(bias, coef_in[:, 0, :], 0.1, sinr, ALU.mult, ALU.add))
            assert done[0] == COEF_STEPS + COEF_LAST

            def third_norm(q):
                at_least(dve, x3T_full, KT * q)
                norm_stats(2, lambda b: batch(QB * q + b), QB, q)
                norm_rows(2, lambda b: batch(QB * q + b), xn3, QB, q)

            def reduce_phase(q, f):
                t, c = FT * q + f + 1, f % 4
                dve.wait_ge(y_ready, t)
                nc.vector.tensor_scalar(n_sb[:, c, :], y_sb[:, c, :], INV_TWO_PI, ROUND, ALU.mult, ALU.add).then_inc(n_ready, 1)
                dve.wait_ge(n_ready, t)
                nc.vector.tensor_scalar(m_sb[:, c, :], n_sb[:, c, :], ROUND, -TWO_PI, ALU.subtract, ALU.mult).then_inc(m_ready, 1)
                dve.wait_ge(m_ready, t)
                nc.vector.tensor_tensor(r_sb[:, c, :], y_sb[:, c, :], m_sb[:, c, :], ALU.add).then_inc(r_ready, 1)
                dve.wait_ge(r_ready, t)
                nc.vector.tensor_scalar(rc_sb[:, c, :], r_sb[:, c, :], PI_BELOW, -PI_BELOW, ALU.min, ALU.max).then_inc(rc_ready, 1)

            def modulate(q, f):
                dve.wait_ge(sin_ready, FT * q + f + 1)
                nc.vector.scalar_tensor_tensor(z_sb[:, f % 4, :], sin_sb[:, f % 4, :], coef[:, AMP, f:f + 1], hid[f % 4][:, :NTOK],
                                               ALU.mult, ALU.add).then_inc(z_ready, 1)

            def finish(q):
                dve.wait_ge(out_done, 16 * 2 * (q + 1))
                dve.wait_ge(x2b_ready, q + 1)
                for half in range(2):
                    dve.wait_ge(acc_full, 2 * q + half + 1)
                    nc.vector.tensor_tensor(fin[:, 2 * half:2 * half + 2].rearrange("s b d -> s (b d)"), acc[half][:S, :],
                                            x2b[:, 2 * half:2 * half + 2].rearrange("s b d -> s (b d)"), ALU.add).then_inc(fin_ready, 1)

            def step(q, f, first, last):
                reduce_phase(q, f)
                if f >= 1 or not first:
                    modulate(*((q, f - 1) if f >= 1 else (q - 1, FT - 1)))
                if f == 2 and not first:
                    finish(q - 1)
                if f == 4 and not last:
                    third_norm(q + 1)

            copied(dve, "cross_o", NP)
            third_norm(0)
            for f in range(FT):
                step(0, f, True, False)
            with dve.Fori(1, NQ - 1) as q:
                for f in range(FT):
                    step(q, f, False, False)
            for f in range(FT):
                step(NQ - 1, f, False, True)
            modulate(NQ - 1, FT - 1)
            finish(NQ - 1)

        @block.gpsimd
        def _(pool):
            def set_to(ap, value):
                nc.gpsimd.memset(ap, value).then_inc(consts_set, 1)

            set_to(half_sb[:], -0.5)
            set_to(v_sb[:, :, HD:HD + 1], 1.0)
            set_to(v_sb[:, :, HD + 1:], 0.0)
            set_to(vx_sb[:, :, :, :, HD:HD + 1].rearrange("p b j g c -> p (b j g) c"), 1.0)
            set_to(vx_sb[:, :, :, :, HD + 1:].rearrange("p b j g c -> p (b j g) c"), 0.0)
            pool.wait_ge(consts_set, NSETS)

            def inverse_std(n, nb, p):
                pool.wait_ge(ln_moments[n], nb * (p + 1))
                alone(pool)
                nc.gpsimd.tensor_scalar(vareps[n][:, :nb], moments[n][:, :nb, 1], EPS, None, ALU.add).then_inc(ln_eps[n], 1)
                pool.wait_ge(ln_eps[n], p + 1)
                nc.gpsimd.tensor_tensor(rstd[n][:, :nb], vareps[n][:, :nb], half_sb[:, :nb], ALU.pow).then_inc(ln_rstd[n], 1)

            def mid_low(name, mid, low, left, count):
                nc.gpsimd.tensor_copy(mid, left).then_inc(mid_ready[name], 1)
                pool.wait_ge(mid_ready[name], count)
                nc.gpsimd.tensor_tensor(low, left, mid, ALU.subtract).then_inc(low_ready[name], 1)

            def split_rest(step, i, parts, left, p):
                copied(pool, step, i)
                alone(pool)
                mid_low(step, parts[:, :, 1, :], parts[:, :, 2, :], left[:], p + 1)

            def split_keys(i, b):
                mid_low("kx", kx_parts[:64, 1, b, :], kx_parts[:64, 2, b, :], kx_rest[:64, b, :], PAIR * (i + 1) + b + 1)

            def body(i, odd):
                if on("next", i):
                    inverse_std(0, PAIR, i + 1)
                if on("self", i):
                    split_keys(i - 1, 1)
                if on("next", i):
                    split_rest("q", i, q_parts, q_rest, i + 1)
                    split_rest("k", i, k_parts, k_rest, i + 1)
                if on("self", i):
                    inverse_std(1, PAIR, i)
                    split_rest("qx", i, qx_parts, qx_rest, i)
                if on("next", i):
                    copied(pool, "kv0", i)
                    alone(pool)
                    split_keys(i, 0)
                    copied(pool, "kv1", i)
                    alone(pool)

            body(-1, 1)
            passes(pool, body)

            pool.wait_ge(ffn_weights_in, 16 * NFFN)
            copied(pool, "cross_o", NP)

            def feed(q):
                inverse_std(2, QB, q)
                at_least(pool, fin_ready, 2 * q)
                for b in range(QB):
                    last = nc.gpsimd.tensor_tensor(x2b[:, b, :], kept[:, bass.ds(QB * q + b, 1), :].rearrange("s o d -> s (o d)"), b2_sb[:], ALU.add)
                last.then_inc(x2b_ready, 1)
            feed(0)
            with pool.Fori(1, NQ) as q:
                feed(q)


def kernel(**inputs):
    import concourse.bacc as _bacc
    from concourse.bass_utils import run_bass_kernel_spmd as _run

    a = {k: np.asarray(v) for k, v in inputs.items()}
    q, k = np.arange(S)[:, None], np.arange(S)[None, :]
    causal = np.where(k > q, np.float32(MASKED), np.float32(0))

    def by_dim(w, heads):
        return w.reshape(w.shape[0], -1, heads, HD).transpose(0, 1, 3, 2).reshape(w.shape)

    arrays = {
        "x": a["x"],
        "ctxT": a["ctx_1024"].transpose(0, 2, 1),
        "wq": by_dim(a["L0_attn_Wq"], 128 // HD),
        "wkv": np.concatenate([by_dim(a["L0_attn_Wkv"][:, :D], 128 // HD), a["L0_attn_Wkv"][:, D:]], 1), "wo": a["L0_attn_Wo"],
        "cwqT": by_dim(a["L0_xattn_Wq"].T, 128 // HD),
        "cwkvT": np.concatenate([by_dim(a["L0_xattn_Wk"].T, G), a["L0_xattn_Wv"].T], 1),
        "cwoT": a["L0_xattn_Wo"].T,
        "w1": a["L0_ffn_W1"],
        "coefs": np.stack([a[f"L0_ffn_{n}"].reshape(FT, 128).T for n in ("b1", "quantum_phases", "quantum_weights_real", "quantum_weights_imag")], 1),
        "w2": a["L0_ffn_W2"], "b2": a["L0_ffn_b2"],
        "ident": np.eye(128, dtype=np.float32),
        "mask": np.stack([causal, causal.T], 1),
    }
    nc = _bacc.Bacc("TRN2", target_bir_lowering=False, num_devices=1)
    args = []
    for name in arrays:
        arrays[name] = np.ascontiguousarray(arrays[name])
        args.append(nc.dram_tensor(f"{name}_dram", arrays[name].shape, mybir.dt.from_np(arrays[name].dtype), kind="ExternalInput").ap())
    out = nc.dram_tensor("out_dram", (B, S, D), F32, kind="ExternalOutput").ap()
    decoder(nc, *args, out)
    r = _run(nc, [{f"{n}_dram": v for n, v in arrays.items()}], core_ids=[0])
    return r.results[0]["out_dram"]
```

```python
import numpy as np
import concourse.bass as bass
from concourse import mybir
from contextlib import ExitStack

F32 = mybir.dt.float32
BF16 = mybir.dt.bfloat16
ACT = mybir.ActivationFunctionType
ALU = mybir.AluOpType
AX = mybir.AxisListType

B, S, D, H, T, F = 16, 100, 256, 16, 361, 1024
HD = D // H
G = 4
R = H // G
KT = D // 128
PAIR = 2
NP = B // PAIR
N = PAIR * S
NTERM = 6
KROWS = NTERM * HD
KM = KROWS + 2
Q_RUNS = ((0, 3, 0, True), (3, 2, 0, True), (5, 1, 0, False))
K_RUNS = ((0, 3, 0, False), (3, 2, 1, False), (5, 1, 2, False))
TT = (T + 127) // 128
TROWS = [min(128, T - 128 * j) for j in range(TT)]
VW = 32
RS = R * S
SCALE = HD ** -0.5
MASKED = -262144.0
EPS = 1e-5
FT = F // 128
QB = 4
NQ = B // QB
NTOK = QB * S
TWO_PI = float(np.float32(2 * np.pi))
INV_TWO_PI = float(np.float32(1 / (2 * np.pi)))
PI_BELOW = 3.1415925
ROUND = 1.5 * 2.0 ** 23
C1 = 6.28125
C2 = float(2 * np.pi - 6.28125)
COEF_STEPS, COEF_LAST = 10, 5

PJ_USES = [("xT", "next"), ("q", "next"), ("self_t1_0", "self"), ("k", "next"), ("self_t1_1", "self"), ("self_t2", "self"), ("cross_max0", "cross"),
           ("self_o", "self"), ("x1T", "self"), ("cross_max1", "last"), ("cross_t1_0", "cross"), ("cross_max1", "both"), ("qx", "self"), ("v", "next"),
           ("self_max", "next"), ("vx0", "self"), ("cross_t1_1", "cross"),
           ("vx1", "self"), ("cross_t2", "cross"), ("kv0", "next"), ("cross_o", "cross"), ("kv1", "next")]
MX_USES = [(f"cross{u}", "cross") for u in range(PAIR * H)] + [(f"self{u}", "next") for u in range(PAIR * G)]
SC_USES = [(f"self{u}", "self") for u in range(PAIR * G)] + [(f"cross{u}", "cross") for u in range(PAIR * TT * G)]


ROWS = [("unit0", 0)] + [(f"unit{n}", 2) for n in range(1, PAIR * G)] + [("self_t1_1", 3), ("self_t2", 1), ("self_o", 1)]
ROWS += [(f"keys{n}", 1) for n in range(TT * G)] + [("x1T", 1)]
assert sum(n for _, n in ROWS) == PAIR * H


def rows_at(step):
    at = [s for s, _ in ROWS].index(step)
    return sum(n for _, n in ROWS[:at]), ROWS[at][1]


NORM_UNIT = 2
XT_UNIT, Q_UNIT, K_UNIT = 4, 6, 7
SELF_MAX_UNIT = 6


def active(i):
    return [p for p, on in (("next", i < NP - 1), ("self", 0 <= i < NP), ("cross", i >= 1), ("both", 1 <= i < NP), ("first", i == -1), ("last", i == NP)) if on]


def uses_by(uses, banks, n, i):
    return sum(len(range(n, sum(part in active(m) for _, part in uses), banks)) for m in range(-1, i))


def use(uses, banks, step, i):
    m = i if isinstance(i, int) else 1
    at = [s for s, part in uses if part in active(m)].index(step)
    n, before = at % banks, uses_by(uses, banks, at % banks, m) + at // banks
    if isinstance(i, int):
        return n, before
    return n, (i - 1) * len(range(n, sum(part in active(m) for _, part in uses), banks)) + before


def decoder(nc, x, ctxT, wq, wkv, wo, cwqT, cwkvT, cwoT, w1, coefs, w2, b2, ident, mask, out):
    ctx = ExitStack()
    with ctx:
        def sb(name, shape, dt=F32):
            return ctx.enter_context(nc.sbuf_tensor(name, shape, dt))

        def sem(name):
            return ctx.enter_context(nc.semaphore(name))

        qs_dram = nc.dram_tensor("qs_dram", [KT, NTERM, 128, N], BF16, kind="Internal").ap()
        ks_dram = nc.dram_tensor("ks_dram", [KT, NTERM, 128, N], BF16, kind="Internal").ap()
        qx_dram = nc.dram_tensor("qx_dram", [KT, NTERM, 128, N], BF16, kind="Internal").ap()
        kx_dram = nc.dram_tensor("kx_dram", [1, NTERM, G * HD, PAIR * T], BF16, kind="Internal").ap()

        ident_sb = sb("ident_sb", [128, 128])
        ident_bf = sb("ident_bf", [128, 128], BF16)
        mask_bf = sb("mask_bf", [S, R, S], BF16)
        maskT_bf = sb("maskT_bf", [S, R, S], BF16)
        mask_f = sb("mask_f", [S, 2, S])
        wq_sb = sb("wq_sb", [128, KT, D])
        wkv_sb = sb("wkv_sb", [128, KT, 2 * D])
        wo_sb = sb("wo_sb", [128, KT, D])
        cwq_sb = sb("cwq_sb", [128, KT, D])
        cwkv_sb = sb("cwkv_sb", [128, KT, 2 * G * HD])
        cwo_sb = sb("cwo_sb", [128, KT, D])
        w1_sb = sb("w1_sb", [128, KT, F])
        w2_sb = sb("w2_sb", [128, FT, D])
        b2_sb = sb("b2_sb", [S, D])
        exp_table = sb("exp_table", [1, 1])
        half_sb = sb("half_sb", [S, QB])

        xl = sb("xl", [S, PAIR, D])
        xr = sb("xr", [S, PAIR, D])
        kept = sb("kept", [S, B, D])
        stats = [sb(f"stats{n}", [S, QB, 6]) for n in range(3)]
        moments = [sb(f"moments{n}", [S, QB, 2]) for n in range(3)]
        vareps = [sb(f"vareps{n}", [S, QB]) for n in range(3)]
        rstd = [sb(f"rstd{n}", [S, QB]) for n in range(3)]
        xn1 = sb("xn1", [S, PAIR, D])
        xn2 = sb("xn2", [S, PAIR, D])
        xT = sb("xT", [128, KT, N])
        x1T = sb("x1T", [128, KT, N])
        ctxT_sb = sb("ctxT_sb", [128, KT, PAIR, T])
        q_parts = sb("q_parts", [128, KT, 3, N], BF16)
        k_parts = sb("k_parts", [128, KT, 3, N], BF16)
        qx_parts = sb("qx_parts", [128, KT, 3, N], BF16)
        kx_parts = sb("kx_parts", [G * HD, 3, PAIR, T], BF16)
        q_rest = sb("q_rest", [128, KT, N])
        k_rest = sb("k_rest", [128, KT, N])
        qx_rest = sb("qx_rest", [128, KT, N])
        kx_rest = sb("kx_rest", [G * HD, PAIR, T])
        q_stack = sb("q_stack", [128, H, N], BF16)
        k_stack = sb("k_stack", [128, H, N], BF16)
        qx_stack = [sb(f"qx_stack{n}", [128, H, N], BF16) for n in range(2)]
        kx_stack = [sb(f"kx_stack{n}", [128, G, PAIR, T], BF16) for n in range(2)]
        vT = sb("vT", [128, PAIR, T])
        v_sb = sb("v_sb", [S, PAIR * H, VW])
        vx_sb = sb("vx_sb", [128, PAIR, TT, G, VW])
        max_s = sb("max_s", [S, H, PAIR])
        max_x = sb("max_x", [S, PAIR, H])
        ms_parts = sb("ms_parts", [H * PAIR, 2, S], BF16)
        mx_parts = sb("mx_parts", [H, PAIR, 2, S], BF16)
        p_self = sb("p_self", [128, PAIR * G, RS])
        p_cross = sb("p_cross", [128, PAIR * TT * G, RS])
        outT_s = sb("outT_s", [128, PAIR, RS])
        outT_x = sb("outT_x", [128, PAIR, RS])
        recip_s = sb("recip_s", [S, PAIR, R, G])
        recip_x = sb("recip_x", [S, PAIR, R, G])
        o_s = sb("o_s", [S, PAIR, D])
        o_x = sb("o_x", [S, PAIR, D])
        oT_s = sb("oT_s", [128, KT, N])
        oT_x = sb("oT_x", [128, KT, N])

        xn3 = qx_stack[0][:S].rearrange("p h n -> p (h n)").bitcast(F32)[:, :QB * D].rearrange("p (b d) -> p b d", d=D)
        x2b = qx_stack[1][:S].rearrange("p h n -> p (h n)").bitcast(F32)[:, :QB * D].rearrange("p (b d) -> p b d", d=D)
        x3T = outT_s
        yT = outT_x
        coef_in = sb("coef_in", [128, 4, FT])
        coef = sb("coef", [128, 8, FT])
        ANG, COSANG, N1, N2, SINV, COSV, AMP, BIAS = range(8)
        y_sb, n_sb, m_sb, r_sb, rc_sb, sin_sb = (p_cross[:, 4 * n:4 * n + 4, :] for n in range(6))
        z_sb = p_self[:, :4, :]
        stack_f32 = q_stack[:].rearrange("p h n -> p (h n)").bitcast(F32).rearrange("p (f n) -> p f n", n=NTOK)
        act_sb = [p_self[:, 4 + f, :] for f in range(4)] + [stack_f32[:, f, :] for f in range(4)]
        fin = k_stack[:S].rearrange("p h n -> p (h n)").bitcast(F32)[:, :QB * D].rearrange("p (b d) -> p b d", d=D)

        mx = [ctx.enter_context(nc.psum_tensor(f"mx{n}", [128, 512], F32)) for n in range(3)]
        sc = [ctx.enter_context(nc.psum_tensor(f"sc{n}", [128, 512], F32)) for n in range(2)]
        ot = ctx.enter_context(nc.psum_tensor("ot", [128, 512], F32))
        pj = [ctx.enter_context(nc.psum_tensor(f"pj{n}", [128, 512], F32)) for n in range(2)]
        hid = [mx[0], mx[1], mx[2], sc[0]]
        acc = [sc[1], ot]

        ident_in = sem("ident_in")
        mask_in = sem("mask_in")
        wq_in = sem("wq_in")
        wkv_in = sem("wkv_in")
        cwkv_in = sem("cwkv_in")
        attn_weights_in = sem("attn_weights_in")
        ffn_weights_in = sem("ffn_weights_in")
        coefs_in = sem("coefs_in")
        waits_carried = sem("waits_carried")
        consts_set = sem("consts_set")
        masks_set = sem("masks_set")
        xl_in = sem("xl_in")
        xr_in = sem("xr_in")
        ctx_in = sem("ctx_in")
        ln_stats = [sem(f"ln{n}_stats") for n in range(3)]
        ln_moments = [sem(f"ln{n}_moments") for n in range(3)]
        ln_eps = [sem(f"ln{n}_eps") for n in range(3)]
        ln_rstd = [sem(f"ln{n}_rstd") for n in range(3)]
        xn_ready = [sem(f"xn{n}_ready") for n in range(3)]
        pj_full = [sem(f"pj_full{n}") for n in range(2)]
        pj_free = [sem(f"pj_free{n}") for n in range(2)]
        mx_full = [sem(f"mx_full{n}") for n in range(3)]
        mx_free = [sem(f"mx_free{n}") for n in range(3)]
        sc_full = [sem(f"sc_full{n}") for n in range(2)]
        sc_free = [sem(f"sc_free{n}") for n in range(2)]
        ot_full = sem("ot_full")
        ot_free = sem("ot_free")
        split = ("q", "k", "qx", "kx", "self_max", "cross_max")
        high_ready = {n: sem(f"{n}_high") for n in split}
        mid_ready = {n: sem(f"{n}_mid") for n in split}
        low_ready = {n: sem(f"{n}_low") for n in split}
        parts_out = {n: sem(f"{n}_out") for n in split[:4]}
        self_stacks_in = sem("self_stacks_in")
        cross_stacks_in = sem("cross_stacks_in")
        maxima_in = {n: sem(f"{n}_in") for n in ("self_max", "cross_max0", "cross_max1")}
        vT_ready = sem("vT_ready")
        recip_ready = {k: sem(f"{k}_recip") for k in ("self", "cross")}
        coef_step = sem("coef_step")
        coef_sin = sem("coef_sin")
        x3T_full = sem("x3T_full")
        x3T_ready = sem("x3T_ready")
        hid_full = sem("hid_full")
        y_ready = sem("y_ready")
        n_ready = sem("n_ready")
        m_ready = sem("m_ready")
        r_ready = sem("r_ready")
        rc_ready = sem("rc_ready")
        sin_ready = sem("sin_ready")
        z_ready = sem("z_ready")
        act_ready = sem("act_ready")
        acc_full = sem("acc_full")
        yT_ready = sem("yT_ready")
        y_full = sem("y_full")
        fin_ready = sem("fin_ready")
        x2b_ready = sem("x2b_ready")
        out_done = sem("out_done")

        block = ctx.enter_context(nc.Block())
        NSETS = 5
        NATTN, NFFN = 3, 3
        STACKED = 16 * 2
        WRITTEN = 16 * len(Q_RUNS)
        SENT = 16 * 2

        def at_least(eng, s, n):
            if not isinstance(n, int) or n > 0:
                eng.wait_ge(s, n)

        def alone(eng):
            eng.sem_inc(waits_carried, 1)

        def filled(eng, uses, full, step, i):
            n, before = use(uses, len(full), step, i)
            eng.wait_ge(full[n], before + 1)
            return n

        def copied(eng, step, i):
            n, before = use(PJ_USES, 2, step, i)
            eng.wait_ge(pj_free[n], before + 1)

        def on(part, i):
            return part in active(i if isinstance(i, int) else 1)

        def passes(eng, body, before_last=lambda: None):
            body(0, 0)
            with eng.Fori(0, (NP - 2) // 2) as j:
                body(2 * j + 1, 1)
                body(2 * j + 2, 0)
            body(NP - 1, 1)
            before_last()
            body(NP, 0)

        def ot_uses(kind, p, b):
            if kind == "self":
                return b if isinstance(p, int) and p == 0 else 4 * p - 2 + b
            return 4 * p + 2 + b if isinstance(p, int) and p == NP - 1 else 4 * p + 4 + b

        def x3T_bank(q):
            return [mx[2], sc[0]] if isinstance(q, int) and q == 0 else pj

        @block.sync
        def _(sp):
            def wait(s, n):
                at_least(sp, s, n)
                alone(sp)

            def wait_copied(step, i):
                copied(sp, step, i)
                alone(sp)

            def rows(b0, n):
                return x[bass.ds(b0, n)].rearrange("b s d -> s b d")

            def load_ctx(p):
                for b in range(PAIR):
                    sp.dma_start(ctxT_sb[:, :, b, :], ctxT[PAIR * p + b].rearrange("(k p) t -> p k t", p=128)
                                 if isinstance(p, int) else
                                 ctxT[bass.ds(PAIR * p + b, 1)].rearrange("o (k p) t -> p (o k) t", p=128)).then_inc(ctx_in, 16)

            def parts_to_dram(name, parts, dram, runs):
                for at, blocks, part, up in runs:
                    for m in range(dram.shape[0]):
                        src = parts[:, m, part:part + blocks, :] if up else parts[:, m, part:part + 1, :].broadcast_to([parts.shape[0], blocks, parts.shape[3]])
                        sp.dma_start(dram[m, at:at + blocks].rearrange("t p s -> p t s"), src).then_inc(parts_out[name], 16)

            def stack(dst, dram, name, p, done):
                wait(parts_out[name], WRITTEN * dram.shape[0] * (p + 1))
                sp.dma_start(dst[:KROWS], dram.rearrange("m t (d h) s -> (t d) m (h s)", d=HD)).then_inc(done, 16)

            def by_tile(stack):
                return stack[:].rearrange("p (m h) s -> p m (h s)", m=KT)

            def body(i, odd):
                if on("last", i):
                    weights(((w1_sb, w1), (w2_sb, w2)), ffn_weights_in)
                    sp.dma_start(b2_sb[:], b2.partition_broadcast(S)).then_inc(ffn_weights_in, 16)
                if on("next", i) and on("self", i):
                    wait(xn_ready[0], PAIR * (i + 1))
                    sp.dma_start(xl[:], rows(PAIR * (i + 1), PAIR)).then_inc(xl_in, 16)
                if on("self", i):
                    wait(ln_stats[1], PAIR * i)
                    sp.dma_start(xr[:], rows(PAIR * i, PAIR)).then_inc(xr_in, 16)
                if on("self", i):
                    wait(low_ready["kx"], PAIR * (i + 1))
                    wait(cross_stacks_in, STACKED * i)
                    parts_to_dram("kx", kx_parts[:G * HD].rearrange("p t b n -> p t (b n)").unsqueeze(1), kx_dram, K_RUNS)
                    if on("next", i):
                        load_ctx(i + 1)
                if on("next", i):
                    wait(low_ready["q"], i + 2)
                    parts_to_dram("q", q_parts, qs_dram, Q_RUNS)
                if on("cross", i):
                    send_cross_maxima(i, 0, qx_stack[1 - odd])
                if on("next", i):
                    wait(low_ready["k"], i + 2)
                    parts_to_dram("k", k_parts, ks_dram, K_RUNS)
                    if on("self", i):
                        wait(ot_free, ot_uses("self", i, 1) + 1)
                    stack(by_tile(q_stack), qs_dram, "q", i + 1, self_stacks_in)
                    stack(by_tile(k_stack), ks_dram, "k", i + 1, self_stacks_in)
                if on("first", i):
                    weights(((cwkv_sb, cwkvT),), cwkv_in)
                    load_ctx(0)
                    weights(((wo_sb, wo), (cwq_sb, cwqT), (cwo_sb, cwoT)), attn_weights_in)
                if on("cross", i):
                    send_cross_maxima(i, 1, qx_stack[1 - odd])
                if on("self", i):
                    wait(low_ready["qx"], i + 1)
                    parts_to_dram("qx", qx_parts, qx_dram, Q_RUNS)
                    stack(by_tile(qx_stack[odd]), qx_dram, "qx", i, cross_stacks_in)
                    stack(kx_stack[odd][:].rearrange("p g b n -> p (g b n)").unsqueeze(1), kx_dram, "kx", i, cross_stacks_in)

                if on("next", i):
                    wait(high_ready["self_max"], i + 2)
                    send_maxima("self_max", i, q_stack, slice(0, N), ms_parts[:])

            def send_cross_maxima(i, b, dst):
                wait(high_ready["cross_max"], PAIR * (i - 1) + b + 1)
                send_maxima(f"cross_max{b}", i, dst, slice(b * S, (b + 1) * S), mx_parts[:, b])

            def send_maxima(step, i, dst, tokens, parts):
                for t in range(2):
                    if t == 1:
                        wait_copied(step, i)
                    sp.dma_start(dst[KROWS + t:KROWS + t + 1, :, tokens], parts[:, t, :]).then_inc(maxima_in[step], 16)

            def weights(pairs, done):
                for dst, src in pairs:
                    sp.dma_start(dst[:], src.rearrange("(k p) n -> p k n", p=128)).then_inc(done, 16)

            sp.sem_inc(out_done, 16 * 2)
            sp.dma_start(xl[:], rows(0, PAIR)).then_inc(xl_in, 16)
            sp.dma_start(ident_sb[:], ident).then_inc(ident_in, 16)
            weights(((wq_sb, wq),), wq_in)
            sp.dma_start(mask_f[:], mask).then_inc(mask_in, 16)
            weights(((wkv_sb, wkv),), wkv_in)
            sp.dma_start(coef_in[:], coefs).then_inc(coefs_in, 16)
            body(-1, 1)
            passes(sp, body)

            def store(q):
                for half in range(2):
                    wait(fin_ready, 2 * q + half + 1)
                    sp.dma_start(out[bass.ds(QB * q + 2 * half, 2)].rearrange("b s d -> s b d"), fin[:, 2 * half:2 * half + 2]).then_inc(out_done, 16)
            with sp.Fori(0, NQ) as q:
                store(q)
            wait(out_done, 16 * 2 * (NQ + 1))

        @block.tensor
        def _(pe):
            def first(i, s, n):
                if on("first", i):
                    pe.wait_ge(s, n)

            def bank(step, i):
                n, before = use(PJ_USES, 2, step, i)
                at_least(pe, pj_free[n], before)
                return pj[n], pj_full[n]

            def transpose_rows(step, i, src):
                into, full = bank(step, i)
                for k in range(KT):
                    for b in range(PAIR):
                        last = nc.tensor.transpose(into[:, k * N + b * S:k * N + (b + 1) * S], src[:, b, k * 128:(k + 1) * 128], ident_sb[:S, :S])
                last.then_inc(full, 1)

            def project_T(step, i, w, srcT, read_step):
                into, full = bank(step, i)
                copied(pe, read_step, i)
                for m in range(KT):
                    for k in range(KT):
                        last = nc.tensor.matmul(into[:, m * N:(m + 1) * N], w[:, k, m * 128:(m + 1) * 128], srcT[:, k, :], start=(k == 0), stop=(k == KT - 1))
                last.then_inc(full, 1)

            def project_rows(step, i, w, srcT, read_step):
                into, full = bank(step, i)
                copied(pe, read_step, i)
                for b in range(PAIR):
                    for k in range(KT):
                        last = nc.tensor.matmul(into[:S, b * D:(b + 1) * D], srcT[:, k, b * S:(b + 1) * S], w[:, k, :], start=(k == 0), stop=(k == KT - 1))
                last.then_inc(full, 1)

            def kv_cross(i, b):
                first(i, cwkv_in, 16)
                pe.wait_ge(ctx_in, 16 * PAIR * (i + 2))
                into, full = bank(f"kv{b}", i)
                for k in range(KT):
                    last = nc.tensor.matmul(into[:, :T], cwkv_sb[:, k, :], ctxT_sb[:, k, b, :], start=(k == 0), stop=(k == KT - 1))
                last.then_inc(full, 1)

            def v_cross(i, b):
                pe.wait_ge(vT_ready, PAIR * i + b + 1)
                into, full = bank(f"vx{b}", i)
                alone(pe)
                for j in range(TT):
                    last = nc.tensor.transpose(into[:TROWS[j], j * 64:(j + 1) * 64], vT[64:, b, j * 128:j * 128 + TROWS[j]], ident_sb[64:, 64:])
                last.then_inc(full, 1)

            def self_rows(i, start, count):
                if not on("next", i):
                    return
                if start == 0:
                    first(i, masks_set, 1)
                    pe.wait_ge(self_stacks_in, STACKED * (i + 2))
                for u in range(start, start + count):
                    b, g = divmod(u, G)
                    n, before = use(MX_USES, 3, f"self{u}", i)
                    at_least(pe, mx_free[n], before)
                    nc.tensor.matmul(mx[n][:S, :RS], ident_bf[:S, :S], mask_bf[:].rearrange("q h k -> q (h k)"), start=True, stop=False, skip_group_check=True)
                    for r in range(R):
                        h = g * R + r
                        last = nc.tensor.matmul(mx[n][:S, r * S:(r + 1) * S], q_stack[:KROWS, h, b * S:(b + 1) * S],
                                                k_stack[:KROWS, h, b * S:(b + 1) * S], start=False, stop=(r == R - 1), skip_group_check=True)
                    last.then_inc(mx_full[n], 1)

            def cross_rows(i, odd, *steps):
                if not on("cross", i):
                    return
                for u in (u for step in steps for u in range(rows_at(step)[0], sum(rows_at(step)))):
                    if u == 0:
                        pe.wait_ge(cross_stacks_in, STACKED * i)
                    b, h = divmod(u, H)
                    n, before = use(MX_USES, 3, f"cross{u}", i)
                    at_least(pe, mx_free[n], before)
                    nc.tensor.matmul(mx[n][:S, :T], qx_stack[1 - odd][:KROWS, h, b * S:(b + 1) * S], kx_stack[1 - odd][:KROWS, h // R, b, :],
                                     start=True, stop=True).then_inc(mx_full[n], 1)

            def maxima_T(step, i, src, last_unit):
                into, full = bank(step, i)
                n, before = use(MX_USES, 3, last_unit, i)
                pe.wait_ge(mx_free[n], before + 1)
                nc.tensor.transpose(into[:src.shape[1], :S], src, ident_sb[:S, :S]).then_inc(full, 1)

            def self_keys(i, between):
                pe.wait_ge(maxima_in["self_max"], SENT * (i + 1))

                def scores(u):
                    b, g = divmod(u, G)
                    n, before = use(SC_USES, 2, f"self{u}", i)
                    at_least(pe, sc_free[n], before)
                    nc.tensor.matmul(sc[n][:S, :RS], ident_bf[:S, :S], maskT_bf[:].rearrange("k h q -> k (h q)"), start=True, stop=False, skip_group_check=True)
                    for r in range(R):
                        h = g * R + r
                        last = nc.tensor.matmul(sc[n][:S, r * S:(r + 1) * S], k_stack[:KM, h, b * S:(b + 1) * S],
                                                q_stack[:KM, h, b * S:(b + 1) * S], start=False, stop=(r == R - 1), skip_group_check=True)
                    last.then_inc(sc_full[n], 1)

                def values(u):
                    b, g = divmod(u, G)
                    n, before = use(SC_USES, 2, f"self{u}", i)
                    pe.wait_ge(sc_free[n], before + 1)
                    if g == 0:
                        at_least(pe, ot_free, ot_uses("self", i, b))
                    for r in range(R):
                        last = nc.tensor.matmul(ot[g * VW:(g + 1) * VW, r * S:(r + 1) * S], v_sb[:, b * H + g * R + r, :],
                                                p_self[:S, u, r * S:(r + 1) * S], start=True, stop=True)
                    if g == G - 1:
                        last.then_inc(ot_full, 1)

                for u in range(PAIR * G + 1):
                    if u < PAIR * G:
                        scores(u)
                        between(u)
                    if u >= 1:
                        values(u - 1)

            def cross_keys(i, odd, b, between):
                pe.wait_ge(maxima_in[f"cross_max{b}"], SENT * i)

                def scores(j, g):
                    n, before = use(SC_USES, 2, f"cross{(b * TT + j) * G + g}", i)
                    at_least(pe, sc_free[n], before)
                    nc.tensor.matmul(sc[n][:TROWS[j], :RS].rearrange("p (r s) -> p r s", r=R), kx_stack[1 - odd][:KM, g, b, j * 128:j * 128 + TROWS[j]],
                                     qx_stack[1 - odd][:KM, g * R:(g + 1) * R, b * S:(b + 1) * S], start=True, stop=True).then_inc(sc_full[n], 1)

                def values(j, g):
                    u = (b * TT + j) * G + g
                    n, before = use(SC_USES, 2, f"cross{u}", i)
                    pe.wait_ge(sc_free[n], before + 1)
                    last = nc.tensor.matmul(ot[g * VW:(g + 1) * VW, :RS], vx_sb[:TROWS[j], b, j, g, :], p_cross[:TROWS[j], u, :],
                                            start=(j == 0), stop=(j == TT - 1))
                    if j == TT - 1 and g == G - 1:
                        last.then_inc(ot_full, 1)

                units = [(j, g) for j in range(TT) for g in range(G)]
                for n, (j, g) in enumerate(units):
                    scores(j, g)
                    between(n)
                    if n % G == 1 and n > G:
                        if n == G + 1:
                            pe.wait_ge(ot_free, ot_uses("cross", i - 1, b))
                        for m in range(n - 1 - G, n - 1):
                            values(*units[m])
                for m in range(len(units) - G, len(units)):
                    values(*units[m])

            def heads_to_rows(kind, i, b, outT, p):
                into, full = bank(f"{kind}_t1_{b}", i)
                pe.wait_ge(ot_free, ot_uses(kind, p, b) + 1)
                for r in range(R):
                    last = nc.tensor.transpose(into[:S, r * 128:(r + 1) * 128], outT[:, b, r * S:(r + 1) * S], ident_sb[:])
                last.then_inc(full, 1)

            def third_T(q):
                pe.wait_ge(xn_ready[2], QB * (q + 1))
                for k in range(KT):
                    for b in range(QB):
                        last = nc.tensor.transpose(x3T_bank(q)[k][:, b * S:(b + 1) * S], xn3[:, b, k * 128:(k + 1) * 128], ident_sb[:S, :S])
                    last.then_inc(x3T_full, 1)

            def hidden(q, f):
                if f == 0:
                    pe.wait_ge(x3T_ready, KT * (q + 1))
                at_least(pe, z_ready, FT * q + f - 3)
                for k in range(KT):
                    last = nc.tensor.matmul(hid[f % 4][:, :NTOK], w1_sb[:, k, f * 128:(f + 1) * 128], x3T[:, k, :], start=(k == 0), stop=(k == KT - 1))
                last.then_inc(hid_full, 1)

            def body(i, odd):
                def first_steps(u):
                    if on("next", i) and u == XT_UNIT:
                        pe.wait_ge(xn_ready[0], PAIR * (i + 2))
                        transpose_rows("xT", i, xn1)
                    if on("next", i) and u == Q_UNIT:
                        first(i, wq_in, 16)
                        project_T("q", i, wq_sb, xT, "xT")
                    if on("self", i) and u == 6:
                        heads_to_rows("self", i, 0, outT_s, i)
                    if on("next", i) and u == K_UNIT:
                        first(i, wkv_in, 16)
                        project_T("k", i, wkv_sb, xT, "xT")
                    cross_rows(i, odd, f"unit{u}")

                if on("self", i):
                    self_keys(i, first_steps)
                else:
                    for u in range(PAIR * G):
                        first_steps(u)
                if on("self", i):
                    heads_to_rows("self", i, 1, outT_s, i)
                cross_rows(i, odd, "self_t1_1")
                if on("self", i):
                    for b in range(PAIR):
                        copied(pe, f"self_t1_{b}", i)
                    transpose_rows("self_t2", i, o_s)
                if on("cross", i):
                    maxima_T("cross_max0", i, max_x[:, 0, :], f"cross{H - 1}")
                cross_rows(i, odd, "self_t2")
                if on("self", i):
                    project_rows("self_o", i, wo_sb, oT_s, "self_t2")
                cross_rows(i, odd, "self_o")
                if on("last", i):
                    cross_rows(i, odd, *(f"keys{n}" for n in range(TT * G)), "x1T")
                    maxima_T("cross_max1", i, max_x[:, 1, :], f"cross{2 * H - 1}")
                if on("cross", i):
                    cross_keys(i, odd, 0, lambda n: cross_rows(i, odd, f"keys{n}") if on("self", i) else None)
                if on("self", i):
                    pe.wait_ge(xn_ready[1], PAIR * (i + 1))
                    transpose_rows("x1T", i, xn2)
                    cross_rows(i, odd, "x1T")
                if on("cross", i):
                    heads_to_rows("cross", i, 0, outT_x, i - 1)
                if on("both", i):
                    maxima_T("cross_max1", i, max_x[:, 1, :], f"cross{2 * H - 1}")
                if on("self", i):
                    project_T("qx", i, cwq_sb, x1T, "x1T")
                if on("next", i):
                    project_rows("v", i, wkv_sb[:, :, D:], xT, "xT")
                self_rows(i, 0, PAIR * G - SELF_MAX_UNIT)

                def self_maxima(n):
                    if n < SELF_MAX_UNIT:
                        self_rows(i, PAIR * G - SELF_MAX_UNIT + n, 1)
                    if on("next", i) and n == SELF_MAX_UNIT:
                        maxima_T("self_max", i, max_s[:].rearrange("s h b -> s (h b)"), f"self{PAIR * G - 1}")

                if on("cross", i):
                    cross_keys(i, odd, 1, self_maxima)
                else:
                    for n in range(SELF_MAX_UNIT + 1):
                        self_maxima(n)
                if on("self", i):
                    v_cross(i, 0)
                if on("cross", i):
                    heads_to_rows("cross", i, 1, outT_x, i - 1)
                if on("self", i):
                    v_cross(i, 1)
                if on("last", i):
                    pe.wait_ge(ffn_weights_in, 16 * NFFN)
                    for uses, free in ((MX_USES, mx_free), (SC_USES, sc_free)):
                        for n in range(len(free)):
                            pe.wait_ge(free[n], uses_by(uses, len(free), n, NP + 1))
                    third_T(0)
                if on("cross", i):
                    for b in range(PAIR):
                        copied(pe, f"cross_t1_{b}", i)
                    transpose_rows("cross_t2", i, o_x)
                if on("last", i):
                    for f in range(2):
                        hidden(0, f)
                if on("next", i):
                    kv_cross(i, 0)
                if on("cross", i):
                    project_rows("cross_o", i, cwo_sb, oT_x, "cross_t2")
                if on("next", i):
                    kv_cross(i, 1)

            pe.wait_ge(ident_in, 16)
            pe.wait_ge(consts_set, NSETS)
            body(-1, 1)
            pe.wait_ge(attn_weights_in, 16 * NATTN)
            passes(pe, body)

            for n in range(len(pj_free)):
                pe.wait_ge(pj_free[n], uses_by(PJ_USES, len(pj_free), n, NP + 1))

            def output(q, f):
                pe.wait_ge(act_ready, FT * q + f + 1)
                if f == 0:
                    at_least(pe, yT_ready, KT * q)
                for m in range(KT):
                    last = nc.tensor.matmul(acc[m][:, :NTOK], w2_sb[:, f, m * 128:(m + 1) * 128], act_sb[f], start=(f == 0), stop=(f == FT - 1))
                    if f == FT - 1:
                        last.then_inc(acc_full, 1)

            def result_rows(q):
                pe.wait_ge(yT_ready, KT * (q + 1))
                for half in range(2):
                    for b in range(2):
                        for m in range(KT):
                            last = nc.tensor.transpose(pj[half][:S, b * D + m * 128:b * D + (m + 1) * 128],
                                                       yT[:, m, (2 * half + b) * S:(2 * half + b + 1) * S], ident_sb[:])
                    last.then_inc(y_full, 1)

            for f in range(FT):
                if f >= 2:
                    hidden(0, f)
                if 3 <= f < FT - 1:
                    output(0, f - 3)
            with pe.Fori(1, NQ) as q:
                third_T(q)
                output(q - 1, FT - 4)
                for f in range(FT):
                    hidden(q, f)
                    if f == 4:
                        result_rows(q - 1)
                    if f < 3:
                        output(q - 1, FT + f - 3)
                    elif f < FT - 1:
                        output(q, f - 3)
            for f in range(FT - 4, FT):
                output(NQ - 1, f)
            result_rows(NQ - 1)

        @block.scalar
        def _(act):
            def copy_T(step, i, dst):
                n = filled(act, PJ_USES, pj_full, step, i)
                nc.scalar.copy(dst[:].rearrange("p k n -> p (k n)"), pj[n][:, :KT * N]).then_inc(pj_free[n], 1)

            def high(step, i, name, parts, p):
                n = filled(act, PJ_USES, pj_full, step, i)
                at_least(act, parts_out[name], WRITTEN * KT * p)
                nc.scalar.copy(parts[:, :, 0, :], pj[n][:, :KT * N].rearrange("p (m n) -> p m n", m=KT)).then_inc(high_ready[name], 1)

            def max_high(name, step, i, part):
                n = filled(act, PJ_USES, pj_full, step, i)
                nc.scalar.copy(part, pj[n][:part.shape[0], :S]).then_inc(high_ready[name], 1)

            def copy_v(i):
                n = filled(act, PJ_USES, pj_full, "v", i)
                nc.scalar.copy(v_sb[:, :, :HD], pj[n][:S, :].rearrange("s (h d) -> s h d", d=HD)).then_inc(pj_free[n], 1)

            def copy_kv(i, b):
                if b == 0:
                    at_least(act, parts_out["kx"], WRITTEN * (i + 1))
                n = filled(act, PJ_USES, pj_full, f"kv{b}", i)
                nc.scalar.copy(vT[64:, b, :], pj[n][64:, :T]).then_inc(vT_ready, 1)
                nc.scalar.copy(kx_parts[:64, 0, b, :], pj[n][:64, :T]).then_inc(high_ready["kx"], 1)

            def copy_vx(i, b):
                n = filled(act, PJ_USES, pj_full, f"vx{b}", i)
                v = pj[n][:, :TT * 64].rearrange("t (j g d) -> t j g d", g=G, d=HD)
                nc.scalar.copy(vx_sb[:, b, 0, :, :HD], v[:, 0])
                nc.scalar.copy(vx_sb[:, b, 1, :, :HD], v[:, 1])
                nc.scalar.copy(vx_sb[:TROWS[2], b, 2, :, :HD], v[:TROWS[2], 2]).then_inc(pj_free[n], 1)

            def self_exps(i, first, last):
                for u in range(first, last):
                    n = filled(act, SC_USES, sc_full, f"self{u}", i)
                    nc.scalar.activation(p_self[:S, u, :], sc[n][:S, :RS], ACT.Exp, scale=SCALE).then_inc(sc_free[n], 1)

            def cross_exps(i, b, first, last):
                for u in range(b * TT * G + first, b * TT * G + last):
                    rows = TROWS[u // G % TT]
                    n = filled(act, SC_USES, sc_full, f"cross{u}", i)
                    nc.scalar.activation(p_cross[:rows, u, :], sc[n][:rows, :RS], ACT.Exp, scale=SCALE).then_inc(sc_free[n], 1)

            def copy_out(kind, p, b, dst):
                act.wait_ge(ot_full, ot_uses(kind, p, b) + 1)
                nc.scalar.copy(dst[:, b, :], ot[:, :RS]).then_inc(ot_free, 1)

            def copy_x3T(q):
                for k in range(KT):
                    act.wait_ge(x3T_full, KT * q + k + 1)
                    nc.scalar.copy(x3T[:, k, :], x3T_bank(q)[k][:, :NTOK]).then_inc(x3T_ready, 1)

            def body(i, odd):
                for u in range(PAIR * G):
                    if on("self", i):
                        self_exps(i, u, u + 1)
                    if on("next", i) and u == XT_UNIT:
                        copy_T("xT", i, xT)
                    if on("next", i) and u == Q_UNIT:
                        high("q", i, "q", q_parts, i + 1)
                    if on("self", i) and u == G:
                        copy_out("self", i, 0, outT_s)
                    if on("next", i) and u == K_UNIT:
                        high("k", i, "k", k_parts, i + 1)
                if on("first", i):
                    act.wait_ge(coef_step, COEF_STEPS)
                    nc.scalar.activation(coef[:, SINV:COSV + 1, :], coef[:, ANG:COSANG + 1, :], ACT.Sin).then_inc(coef_sin, 1)
                    nc.scalar.activation(exp_table[:], half_sb[:1, :1], ACT.Exp)
                if on("self", i):
                    copy_out("self", i, 1, outT_s)
                    copy_T("self_t2", i, oT_s)
                if on("cross", i):
                    max_high("cross_max", "cross_max0", i, mx_parts[:, 0, 0, :])
                if on("last", i):
                    max_high("cross_max", "cross_max1", i, mx_parts[:, 1, 0, :])
                if on("cross", i):
                    cross_exps(i, 0, 0, TT * G)
                    copy_out("cross", i - 1, 0, outT_x)
                if on("self", i):
                    copy_T("x1T", i, x1T)
                if on("both", i):
                    max_high("cross_max", "cross_max1", i, mx_parts[:, 1, 0, :])
                if on("self", i):
                    high("qx", i, "qx", qx_parts, i)
                if on("next", i):
                    copy_v(i)
                if on("cross", i):
                    cross_exps(i, 1, 0, SELF_MAX_UNIT + 1)
                if on("next", i):
                    max_high("self_max", "self_max", i, ms_parts[:, 0, :])
                if on("cross", i):
                    cross_exps(i, 1, SELF_MAX_UNIT + 1, TT * G)
                    copy_out("cross", i - 1, 1, outT_x)
                if on("self", i):
                    copy_vx(i, 0)
                    copy_vx(i, 1)
                if on("last", i):
                    copy_x3T(0)
                if on("cross", i):
                    copy_T("cross_t2", i, oT_x)
                if on("next", i):
                    copy_kv(i, 0)
                    copy_kv(i, 1)

            act.wait_ge(consts_set, NSETS)
            body(-1, 1)
            passes(act, body)

            act.wait_ge(coef_step, COEF_STEPS + COEF_LAST)

            def phase(q, f):
                act.wait_ge(hid_full, FT * q + f + 1)
                nc.scalar.activation(y_sb[:, f % 4, :], hid[f % 4][:, :NTOK], ACT.Identity, bias=coef[:, BIAS, f:f + 1], scale=0.1).then_inc(y_ready, 1)

            def sine(q, f):
                act.wait_ge(rc_ready, FT * q + f + 1)
                nc.scalar.activation(sin_sb[:, f % 4, :], rc_sb[:, f % 4, :], ACT.Sin).then_inc(sin_ready, 1)

            def relu(q, f):
                act.wait_ge(z_ready, FT * q + f + 1)
                nc.scalar.activation(act_sb[f], z_sb[:, f % 4, :], ACT.Relu, bias=coef_in[:, 0, f:f + 1]).then_inc(act_ready, 1)

            def copy_result(q):
                for m in range(KT):
                    act.wait_ge(acc_full, KT * q + m + 1)
                    nc.scalar.copy(yT[:, m, :], acc[m][:, :NTOK]).then_inc(yT_ready, 1)

            def step(q, f, first):
                if f == 0 and not first:
                    copy_x3T(q)
                    sine(q - 1, FT - 2)
                    relu(q - 1, FT - 3)
                if f == 3 and not first:
                    copy_result(q - 1)
                phase(q, f)
                if f < FT - 1:
                    if f >= 1 or not first:
                        sine(*((q, f - 1) if f >= 1 else (q - 1, FT - 1)))
                    if f >= 2 or not first:
                        relu(*((q, f - 2) if f >= 2 else (q - 1, FT + f - 2)))

            for f in range(FT):
                step(0, f, True)
            with act.Fori(1, NQ) as q:
                for f in range(FT):
                    step(q, f, False)
            sine(NQ - 1, FT - 2)
            relu(NQ - 1, FT - 3)
            sine(NQ - 1, FT - 1)
            relu(NQ - 1, FT - 2)
            relu(NQ - 1, FT - 1)
            copy_result(NQ - 1)

        @block.vector
        def _(dve):
            def batch(b):
                return kept[:, b, :] if isinstance(b, int) else kept[:, bass.ds(b, 1), :].rearrange("s o d -> s (o d)")

            def norm_stats(n, src, nb, p):
                for b in range(nb):
                    nc.vector.bn_stats(stats[n][:, b, :], src(b)).then_inc(ln_stats[n], 1)
                for b in range(nb):
                    dve.wait_ge(ln_stats[n], nb * p + b + 1)
                    alone(dve)
                    nc.vector.bn_aggr(moments[n][:, b, :], stats[n][:, b, :]).then_inc(ln_moments[n], 1)

            def norm_rows(n, src, dst, nb, p):
                dve.wait_ge(ln_rstd[n], p + 1)
                dve.wait_ge(ln_moments[n], nb * (p + 1))
                for b in range(nb):
                    nc.vector.tensor_scalar(dst[:, b, :], src(b), moments[n][:, b, 0:1], rstd[n][:, b:b + 1], ALU.subtract, ALU.mult).then_inc(xn_ready[n], 1)

            def rest(step, i, name, parts, dst, p):
                n, before = use(PJ_USES, 2, step, i)
                dve.wait_ge(high_ready[name], p + 1)
                at_least(dve, low_ready[name], p)
                nc.vector.tensor_tensor(dst[:], pj[n][:, :KT * N].rearrange("p (m n) -> p m n", m=KT), parts[:, :, 0, :], ALU.subtract).then_inc(pj_free[n], 1)

            def rest_kv(i, b):
                n, before = use(PJ_USES, 2, f"kv{b}", i)
                dve.wait_ge(high_ready["kx"], PAIR * (i + 1) + b + 1)
                at_least(dve, low_ready["kx"], PAIR * (i + 1))
                nc.vector.tensor_tensor(kx_rest[:64, b, :], pj[n][:64, :T], kx_parts[:64, 0, b, :], ALU.subtract).then_inc(pj_free[n], 1)

            def second_part(name, step, i, parts, made):
                n, before = use(PJ_USES, 2, step, i)
                dve.wait_ge(high_ready[name], made)
                nc.vector.tensor_tensor(parts[:, 1, :], pj[n][:parts.shape[0], :S], parts[:, 0, :], ALU.subtract).then_inc(pj_free[n], 1)

            def self_maxima(i):
                for u in range(PAIR * G):
                    b, g = divmod(u, G)
                    n = filled(dve, MX_USES, mx_full, f"self{u}", i)
                    nc.vector.reduce_max(max_s[:, g * R:(g + 1) * R, b], mx[n][:S, :RS].rearrange("q (r k) -> q r k", r=R), AX.X).then_inc(mx_free[n], 1)

            def cross_maxima(i, *steps):
                for u in (u for step in steps for u in range(rows_at(step)[0], sum(rows_at(step)))) if on("cross", i) else ():
                    b, h = divmod(u, H)
                    n = filled(dve, MX_USES, mx_full, f"cross{u}", i)
                    nc.vector.reduce_max(max_x[:, b, h:h + 1], mx[n][:S, :T], AX.X).then_inc(mx_free[n], 1)

            def normalise(kind, i, b, recip, o, p):
                n = filled(dve, PJ_USES, pj_full, f"{kind}_t1_{b}", i)
                heads = pj[n][:S, :].rearrange("s (r g c) -> s r g c", g=G, c=VW)
                nc.vector.reciprocal(recip[:, b, :, :], heads[:, :, :, HD]).then_inc(recip_ready[kind], 1)
                dve.wait_ge(recip_ready[kind], PAIR * p + b + 1)
                nc.vector.tensor_tensor(o[:, b, :].rearrange("s (g r d) -> s r g d", g=G, r=R), heads[:, :, :, :HD],
                                        recip[:, b, :, :].unsqueeze(3).broadcast_to([S, R, G, HD]), ALU.mult).then_inc(pj_free[n], 1)

            def residual(step, i, p, src):
                n = filled(dve, PJ_USES, pj_full, step, i)
                nc.vector.tensor_tensor(kept[:, bass.ds(PAIR * p, PAIR), :].rearrange("s b d -> s (b d)"), pj[n][:S, :], src.rearrange("s b d -> s (b d)"),
                                        ALU.add).then_inc(pj_free[n], 1)

            def masks():
                dve.wait_ge(ident_in, 16)
                nc.vector.tensor_copy(ident_bf[:], ident_sb[:])
                dve.wait_ge(mask_in, 16)
                for r in range(R):
                    nc.vector.tensor_copy(mask_bf[:, r, :], mask_f[:, 0, :])
                    last = nc.vector.tensor_copy(maskT_bf[:, r, :], mask_f[:, 1, :])
                last.then_inc(masks_set, 1)

            steps_done = [0]

            def then(ins):
                steps_done[0] += 1
                ins.then_inc(coef_step, 1)
                dve.wait_ge(coef_step, steps_done[0])

            ph, sinr, cosr = coef_in[:, 1, :], coef[:, ANG, :], coef[:, COSANG, :]
            n1, n2 = coef[:, N1, :], coef[:, N2, :]

            def set_once():
                for stack in (k_stack, *kx_stack):
                    nc.vector.memset(stack[KROWS:KM], -1.0)
                dve.wait_ge(coefs_in, 16)
                then(nc.vector.tensor_scalar(n1, ph, INV_TWO_PI, ROUND, ALU.mult, ALU.add))
                then(nc.vector.tensor_scalar(n2, n1, ROUND, None, ALU.subtract))
                then(nc.vector.scalar_tensor_tensor(sinr, n2, -C1, ph, ALU.mult, ALU.add))
                then(nc.vector.scalar_tensor_tensor(cosr, n2, -C2, sinr, ALU.mult, ALU.add))
                then(nc.vector.tensor_scalar(sinr, cosr, PI_BELOW, -PI_BELOW, ALU.min, ALU.max))
                then(nc.vector.tensor_scalar(n1, sinr, float(np.pi / 2), None, ALU.add))
                then(nc.vector.tensor_scalar(n2, n1, INV_TWO_PI, ROUND, ALU.mult, ALU.add))
                then(nc.vector.tensor_scalar(cosr, n2, ROUND, -TWO_PI, ALU.subtract, ALU.mult))
                then(nc.vector.tensor_tensor(n2, cosr, n1, ALU.add))
                then(nc.vector.tensor_scalar(cosr, n2, PI_BELOW, -PI_BELOW, ALU.min, ALU.max))
                assert steps_done[0] == COEF_STEPS
                dve.wait_ge(coef_sin, 1)
                then(nc.vector.tensor_tensor(n1, coef[:, COSV, :], coef_in[:, 2, :], ALU.mult))
                then(nc.vector.tensor_tensor(n2, coef[:, SINV, :], coef_in[:, 3, :], ALU.mult))
                then(nc.vector.tensor_tensor(cosr, n1, n2, ALU.add))
                then(nc.vector.scalar_tensor_tensor(coef[:, AMP, :], cosr, 0.1, coef_in[:, 3, :], ALU.mult, ALU.mult))
                then(nc.vector.scalar_tensor_tensor(coef[:, BIAS, :], coef_in[:, 0, :], 0.1, sinr, ALU.mult, ALU.add))
                assert steps_done[0] == COEF_STEPS + COEF_LAST

            x_of = lambda b: xl[:, b, :]

            def x1_of(i):
                return lambda b: batch(PAIR * i + b)

            def body(i, odd):
                if on("next", i):
                    dve.wait_ge(xl_in, 16 * (i + 2))
                    norm_stats(0, x_of, PAIR, i + 1)
                for u in range(PAIR * G):
                    if on("next", i) and u == NORM_UNIT:
                        norm_rows(0, x_of, xn1, PAIR, i + 1)
                    if on("first", i) and u == 2:
                        masks()
                    if on("next", i) and u == Q_UNIT:
                        rest("q", i, "q", q_parts, q_rest, i + 1)
                    if on("self", i) and u == 6:
                        normalise("self", i, 0, recip_s, o_s, i)
                    if on("next", i) and u == K_UNIT:
                        rest("k", i, "k", k_parts, k_rest, i + 1)
                    if on("first", i) and u == 7:
                        set_once()
                    cross_maxima(i, f"unit{u}")
                if on("self", i):
                    normalise("self", i, 1, recip_s, o_s, i)
                cross_maxima(i, "self_t1_1")
                if on("cross", i):
                    second_part("cross_max", "cross_max0", i, mx_parts[:, 0], PAIR * (i - 1) + 1)
                cross_maxima(i, "self_t2")
                if on("self", i):
                    dve.wait_ge(xr_in, 16 * (i + 1))
                    residual("self_o", i, i, xr[:])
                cross_maxima(i, "self_o")
                if on("self", i):
                    copied(dve, "self_o", i)
                    alone(dve)
                    norm_stats(1, x1_of(i), PAIR, i)
                cross_maxima(i, *(f"keys{n}" for n in range(4)))
                if on("self", i):
                    norm_rows(1, x1_of(i), xn2, PAIR, i)
                cross_maxima(i, *(f"keys{n}" for n in range(4, TT * G)))
                cross_maxima(i, "x1T")
                if on("last", i):
                    second_part("cross_max", "cross_max1", i, mx_parts[:, 1], PAIR * (i - 1) + 2)
                if on("cross", i):
                    normalise("cross", i, 0, recip_x, o_x, i - 1)
                if on("both", i):
                    second_part("cross_max", "cross_max1", i, mx_parts[:, 1], PAIR * (i - 1) + 2)
                if on("self", i):
                    rest("qx", i, "qx", qx_parts, qx_rest, i)
                if on("next", i):
                    self_maxima(i)
                    second_part("self_max", "self_max", i, ms_parts[:], i + 2)
                if on("cross", i):
                    normalise("cross", i, 1, recip_x, o_x, i - 1)
                if on("next", i):
                    rest_kv(i, 0)
                if on("cross", i):
                    residual("cross_o", i, i - 1, kept[:, bass.ds(PAIR * (i - 1), PAIR), :])
                if on("next", i):
                    rest_kv(i, 1)

            body(-1, 1)

            def third_stats(q):
                norm_stats(2, lambda b: batch(QB * q + b), QB, q)

            def third_rows(q):
                at_least(dve, x3T_full, KT * q)
                norm_rows(2, lambda b: batch(QB * q + b), xn3, QB, q)

            def before_last():
                third_stats(0)
                third_rows(0)

            passes(dve, body, before_last)

            def reduce_phase(q, f):
                t, c = FT * q + f + 1, f % 4
                dve.wait_ge(y_ready, t)
                nc.vector.tensor_scalar(n_sb[:, c, :], y_sb[:, c, :], INV_TWO_PI, ROUND, ALU.mult, ALU.add).then_inc(n_ready, 1)
                dve.wait_ge(n_ready, t)
                nc.vector.tensor_scalar(m_sb[:, c, :], n_sb[:, c, :], ROUND, -TWO_PI, ALU.subtract, ALU.mult).then_inc(m_ready, 1)
                dve.wait_ge(m_ready, t)
                nc.vector.tensor_tensor(r_sb[:, c, :], y_sb[:, c, :], m_sb[:, c, :], ALU.add).then_inc(r_ready, 1)
                dve.wait_ge(r_ready, t)
                nc.vector.tensor_scalar(rc_sb[:, c, :], r_sb[:, c, :], PI_BELOW, -PI_BELOW, ALU.min, ALU.max).then_inc(rc_ready, 1)

            def modulate(q, f):
                dve.wait_ge(sin_ready, FT * q + f + 1)
                nc.vector.scalar_tensor_tensor(z_sb[:, f % 4, :], sin_sb[:, f % 4, :], coef[:, AMP, f:f + 1], hid[f % 4][:, :NTOK],
                                               ALU.mult, ALU.add).then_inc(z_ready, 1)

            def finish(q, half):
                if half == 0:
                    dve.wait_ge(out_done, 16 * 2 * (q + 1))
                    dve.wait_ge(x2b_ready, q + 1)
                dve.wait_ge(y_full, 2 * q + half + 1)
                nc.vector.tensor_tensor(fin[:, 2 * half:2 * half + 2].rearrange("s b d -> s (b d)"), pj[half][:S, :],
                                        x2b[:, 2 * half:2 * half + 2].rearrange("s b d -> s (b d)"), ALU.add).then_inc(fin_ready, 1)

            def step(q, f, first, last):
                reduce_phase(q, f)
                if f >= 1 or not first:
                    modulate(*((q, f - 1) if f >= 1 else (q - 1, FT - 1)))
                if f == 2 and not last:
                    third_stats(q + 1)
                if f in (4, 5) and not first:
                    finish(q - 1, f - 4)
                if f == 5 and not last:
                    third_rows(q + 1)

            for f in range(FT):
                step(0, f, True, False)
            with dve.Fori(1, NQ - 1) as q:
                for f in range(FT):
                    step(q, f, False, False)
            for f in range(FT):
                step(NQ - 1, f, False, True)
            modulate(NQ - 1, FT - 1)
            for half in range(2):
                finish(NQ - 1, half)

        @block.gpsimd
        def _(pool):
            def set_to(ap, value):
                nc.gpsimd.memset(ap, value).then_inc(consts_set, 1)

            set_to(half_sb[:], -0.5)
            set_to(v_sb[:, :, HD:HD + 1], 1.0)
            set_to(v_sb[:, :, HD + 1:], 0.0)
            set_to(vx_sb[:, :, :, :, HD:HD + 1].rearrange("p b j g c -> p (b j g) c"), 1.0)
            set_to(vx_sb[:, :, :, :, HD + 1:].rearrange("p b j g c -> p (b j g) c"), 0.0)
            pool.wait_ge(consts_set, NSETS)

            def inverse_std(n, nb, p):
                pool.wait_ge(ln_moments[n], nb * (p + 1))
                alone(pool)
                nc.gpsimd.tensor_scalar(vareps[n][:, :nb], moments[n][:, :nb, 1], EPS, None, ALU.add).then_inc(ln_eps[n], 1)
                pool.wait_ge(ln_eps[n], p + 1)
                nc.gpsimd.tensor_tensor(rstd[n][:, :nb], vareps[n][:, :nb], half_sb[:, :nb], ALU.pow).then_inc(ln_rstd[n], 1)

            def mid_low(name, mid, low, left, count):
                nc.gpsimd.tensor_copy(mid, left).then_inc(mid_ready[name], 1)
                pool.wait_ge(mid_ready[name], count)
                nc.gpsimd.tensor_tensor(low, left, mid, ALU.subtract).then_inc(low_ready[name], 1)

            def split_rest(step, i, parts, left, p):
                copied(pool, step, i)
                alone(pool)
                mid_low(step, parts[:, :, 1, :], parts[:, :, 2, :], left[:], p + 1)

            def split_keys(i, b):
                mid_low("kx", kx_parts[:64, 1, b, :], kx_parts[:64, 2, b, :], kx_rest[:64, b, :], PAIR * (i + 1) + b + 1)

            def body(i, odd):
                if on("next", i):
                    inverse_std(0, PAIR, i + 1)
                if on("self", i):
                    split_keys(i - 1, 1)
                if on("next", i):
                    split_rest("q", i, q_parts, q_rest, i + 1)
                    split_rest("k", i, k_parts, k_rest, i + 1)
                if on("self", i):
                    inverse_std(1, PAIR, i)
                    split_rest("qx", i, qx_parts, qx_rest, i)
                if on("next", i):
                    copied(pool, "kv0", i)
                    alone(pool)
                    split_keys(i, 0)
                    copied(pool, "kv1", i)
                    alone(pool)

            body(-1, 1)
            passes(pool, body, lambda: inverse_std(2, QB, 0))

            pool.wait_ge(ffn_weights_in, 16 * NFFN)
            copied(pool, "cross_o", NP)

            def feed(q):
                at_least(pool, fin_ready, 2 * q)
                for b in range(QB):
                    last = nc.gpsimd.tensor_tensor(x2b[:, b, :], kept[:, bass.ds(QB * q + b, 1), :].rearrange("s o d -> s (o d)"), b2_sb[:], ALU.add)
                last.then_inc(x2b_ready, 1)
            feed(0)
            inverse_std(2, QB, 1)
            with pool.Fori(1, NQ - 1) as q:
                inverse_std(2, QB, q + 1)
                feed(q)
            feed(NQ - 1)


def kernel(**inputs):
    import concourse.bacc as _bacc
    from concourse.bass_utils import run_bass_kernel_spmd as _run

    a = {k: np.asarray(v) for k, v in inputs.items()}
    q, k = np.arange(S)[:, None], np.arange(S)[None, :]
    causal = np.where(k > q, np.float32(MASKED), np.float32(0))

    def by_dim(w, heads):
        return w.reshape(w.shape[0], -1, heads, HD).transpose(0, 1, 3, 2).reshape(w.shape)

    arrays = {
        "x": a["x"],
        "ctxT": a["ctx_1024"].transpose(0, 2, 1),
        "wq": by_dim(a["L0_attn_Wq"], 128 // HD),
        "wkv": np.concatenate([by_dim(a["L0_attn_Wkv"][:, :D], 128 // HD), a["L0_attn_Wkv"][:, D:]], 1), "wo": a["L0_attn_Wo"],
        "cwqT": by_dim(a["L0_xattn_Wq"].T, 128 // HD),
        "cwkvT": np.concatenate([by_dim(a["L0_xattn_Wk"].T, G), a["L0_xattn_Wv"].T], 1),
        "cwoT": a["L0_xattn_Wo"].T,
        "w1": a["L0_ffn_W1"],
        "coefs": np.stack([a[f"L0_ffn_{n}"].reshape(FT, 128).T for n in ("b1", "quantum_phases", "quantum_weights_real", "quantum_weights_imag")], 1),
        "w2": a["L0_ffn_W2"], "b2": a["L0_ffn_b2"],
        "ident": np.eye(128, dtype=np.float32),
        "mask": np.stack([causal, causal.T], 1),
    }
    nc = _bacc.Bacc("TRN2", target_bir_lowering=False, num_devices=1)
    args = []
    for name in arrays:
        arrays[name] = np.ascontiguousarray(arrays[name])
        args.append(nc.dram_tensor(f"{name}_dram", arrays[name].shape, mybir.dt.from_np(arrays[name].dtype), kind="ExternalInput").ap())
    out = nc.dram_tensor("out_dram", (B, S, D), F32, kind="ExternalOutput").ap()
    decoder(nc, *args, out)
    r = _run(nc, [{f"{n}_dram": v for n, v in arrays.items()}], core_ids=[0])
    return r.results[0]["out_dram"]
```
